# Optimizing a Trainium2 kernel written in Bass

```python
import numpy as np
import jax
import jax.numpy as jnp

def _softmax(x, axis=-1):
    return jax.nn.softmax(x, axis=axis)

def _gelu(x):
    return jax.nn.gelu(x, approximate=True)

def _silu(x):
    return jax.nn.silu(x)

def _sigmoid(x):
    return jax.nn.sigmoid(x)

def _layernorm(x, axis=-1, eps=1e-05):
    m = jnp.mean(x, axis=axis, keepdims=True)
    v = jnp.var(x, axis=axis, keepdims=True)
    return (x - m) / jnp.sqrt(v + eps)

def _scatter_add(tgt, idx, src, axis=0):
    return tgt.at[idx].add(src)

def _segment_sum(src, seg, n):
    return jax.ops.segment_sum(src, seg, n)
kernel_name = 'mk_prb_d1_jaxref_r2_013e1a'

def setup_inputs(seed: int=0):
    np.random.seed(seed)
    _w = jnp.asarray

    def _L0_attn_setup():
        import jax, jax.numpy as jnp
        import numpy as np
        H = 2048
        D = H // 4
        key = jax.random.key(seed)
        k1, k2, k3, k4, k5 = jax.random.split(key, 5)
        x = jax.random.normal(k1, (4, 2048, H), dtype=jnp.float32)
        s_in = 1.0 / np.sqrt(H)
        Wqkv = jax.random.normal(k2, (H, 3 * D), dtype=jnp.float32) * s_in
        bqkv = jax.random.normal(k3, (3 * D,), dtype=jnp.float32) * 0.01
        Wo = jax.random.normal(k4, (D, H), dtype=jnp.float32) * (1.0 / np.sqrt(D))
        bo = jax.random.normal(k5, (H,), dtype=jnp.float32) * 0.01
        return {'x': x, 'Wqkv': Wqkv, 'bqkv': bqkv, 'Wo': Wo, 'bo': bo}
    _L0_attn_in = _L0_attn_setup()

    def _L0_ffn_setup():
        import jax, jax.numpy as jnp
        import numpy as np
        IN_F = 2048
        OUT_F = 2048
        RANK = 8
        NUM_EXPERTS = 64
        TOP_K = 16
        ROUTER_DIM = 16
        ALPHA = 32
        SCALING = ALPHA / TOP_K
        BOTTLENECK = NUM_EXPERTS * RANK
        key = jax.random.key(seed)
        ks = jax.random.split(key, 5)
        x = jax.random.normal(ks[0], (4, 2048, IN_F), dtype=jnp.float32)
        bound_a = float(np.sqrt(6.0 / IN_F))
        A_w = jax.random.uniform(ks[1], (BOTTLENECK, IN_F), jnp.float32, -bound_a, bound_a)
        B_w = jax.random.normal(ks[2], (OUT_F, BOTTLENECK), dtype=jnp.float32) * 0.02
        Wq_w = jax.random.normal(ks[3], (ROUTER_DIM, IN_F), dtype=jnp.float32) * 0.02
        keys = jax.random.normal(ks[4], (NUM_EXPERTS, ROUTER_DIM), dtype=jnp.float32) * 0.01
        return {'x': x, 'A_w': A_w, 'B_w': B_w, 'Wq_w': Wq_w, 'keys': keys}
    _L0_ffn_in = _L0_ffn_setup()
    _d = {'L0_attn_x': _L0_attn_in['x'], 'L0_attn_Wqkv': _L0_attn_in['Wqkv'], 'L0_attn_bqkv': _L0_attn_in['bqkv'], 'L0_attn_Wo': _L0_attn_in['Wo'], 'L0_attn_bo': _L0_attn_in['bo'], 'L0_ffn_A_w': _L0_ffn_in['A_w'], 'L0_ffn_B_w': _L0_ffn_in['B_w'], 'L0_ffn_Wq_w': _L0_ffn_in['Wq_w'], 'L0_ffn_keys': _L0_ffn_in['keys']}
    _x0 = _d['L0_attn_x']
    _d['L0_attn_x'] = jax.random.normal(jax.random.fold_in(jax.random.key(seed), 1), (2, 2048, 2048), dtype=_x0.dtype)
    del _x0
    return _d

def reference(L0_attn_x, L0_attn_Wqkv, L0_attn_bqkv, L0_attn_Wo, L0_attn_bo, L0_ffn_A_w, L0_ffn_B_w, L0_ffn_Wq_w, L0_ffn_keys):

    def _L0_attn_ref(x, Wqkv, bqkv, Wo, bo):
        import jax, jax.numpy as jnp
        import numpy as np
        H = 2048
        D = H // 4
        B, S, C = x.shape
        d = C // 4
        qkv = jnp.einsum('bsc,cf->bsf', x, Wqkv) + bqkv
        qkv = qkv.reshape(B, S, 3, d)
        q, k, v = (qkv[:, :, 0], qkv[:, :, 1], qkv[:, :, 2])
        scale = 1.0 / jnp.sqrt(jnp.float32(d)).astype(x.dtype)
        attn = jnp.einsum('bqd,bkd->bqk', q, k) * scale
        attn = jax.nn.softmax(attn, axis=-1)
        out = jnp.einsum('bqk,bkd->bqd', attn, v)
        return jnp.einsum('bqd,dc->bqc', out, Wo) + bo

    def _L0_ffn_ref(x, A_w, B_w, Wq_w, keys):
        import jax, jax.numpy as jnp
        import numpy as np
        IN_F = 2048
        OUT_F = 2048
        RANK = 8
        NUM_EXPERTS = 64
        TOP_K = 16
        ROUTER_DIM = 16
        ALPHA = 32
        SCALING = ALPHA / TOP_K
        BOTTLENECK = NUM_EXPERTS * RANK
        q = jnp.einsum('bsd,rd->bsr', x, Wq_w)
        scores = jnp.einsum('bsr,er->bse', q, keys)
        top_vals, top_idx = jax.lax.top_k(scores, TOP_K)
        top_w = jax.nn.softmax(top_vals, axis=-1)
        gate = jnp.sum(jax.nn.one_hot(top_idx, NUM_EXPERTS, dtype=top_w.dtype) * top_w[..., None], axis=-2)
        z = jnp.einsum('bsd,nd->bsn', x, A_w)
        z = z.reshape(*z.shape[:-1], NUM_EXPERTS, RANK)
        z_gated = (z * gate[..., None]).reshape(*z.shape[:-2], BOTTLENECK)
        out = jnp.einsum('bsn,on->bso', z_gated, B_w) * SCALING
        return out
    x = L0_attn_x
    xn = _layernorm(x, axis=-1)
    x = x + _L0_attn_ref(xn, L0_attn_Wqkv, L0_attn_bqkv, L0_attn_Wo, L0_attn_bo) + _L0_ffn_ref(xn, L0_ffn_A_w, L0_ffn_B_w, L0_ffn_Wq_w, L0_ffn_keys)
    return x

_drawn_inputs = setup_inputs


def setup_inputs(seed=0):
    import zlib

    import numpy as np

    out = dict(_drawn_inputs(seed))
    spreads = {}
    factors = {'L0_attn_bqkv': 5.802, 'L0_attn_bo': 5.737}
    for name, (base, spread) in spreads.items():
        noise = np.random.default_rng([zlib.crc32(name.encode()), seed]).standard_normal(out[name].shape)
        drawn = base * np.exp(spread * noise) if base else spread * noise
        out[name] = jnp.asarray(drawn.astype(out[name].dtype))
    for name, factor in factors.items():
        out[name] = (out[name] * factor).astype(out[name].dtype)
    return out
```

```python
from contextlib import ExitStack

import concourse.bass as bass
from concourse import mybir

ALU = mybir.AluOpType
ACT = mybir.ActivationFunctionType
F32 = mybir.dt.float32
F32R = mybir.dt.float32r
AX = mybir.AxisListType

P = 128
BANKS = 8
W = 512
LOWEST = -3.0e38


def static(v):
    return isinstance(v, int)


def wait(engine, sem, value):
    if static(value) and value <= 0:
        return
    engine.wait_ge(sem, value)


class Chain:

    def __init__(self, engine, sem, base):
        self.engine, self.sem, self.base, self.n = engine, sem, base, 0

    def step(self, instruction):
        self.n += 1
        instruction.then_inc(self.sem, 1)

    def wait(self, back=0):
        self.engine.wait_ge(self.sem, self.base + self.n - back)

    def link(self, instruction):
        self.step(instruction)
        self.wait()


def layer_kernel(nc, x, xT, Wqkv, bqkv, b_cols, Wo, bo, A_T, B_T, WqT, keysT, out):
    T, C = x.shape
    D = Wo.shape[0]
    NE, RD = keysT.shape[1], keysT.shape[0]
    RANK = D // NE
    NB = 2
    S = T // NB
    KT = C // P
    TG = 1024
    NG = T // TG
    QG = 512
    NQ = T // QG
    KEYT = S // P
    DT = D // P
    assert D == W and KT == 16 and KEYT == 16 and DT == 4 and A_T.shape[1] == D

    k_scr = nc.dram_tensor("k_scratch", [D, T], F32, kind="Internal").ap()
    q_scr = nc.dram_tensor("q_scratch", [D, T], F32, kind="Internal").ap()
    z_scr = nc.dram_tensor("z_scratch", [T, D], F32, kind="Internal").ap()
    v_scr = nc.dram_tensor("v_scratch", [T, D], F32, kind="Internal").ap()
    stat_scr = nc.dram_tensor("stat_scratch", [NG, 2, TG], F32, kind="Internal").ap()

    with ExitStack() as whole:
        psum = whole.enter_context(nc.psum_tensor("psum", [P, BANKS, W], F32))
        phase_a(nc, psum, x, xT, Wqkv, bqkv, b_cols, A_T, WqT, keysT, k_scr, q_scr, z_scr, v_scr, stat_scr,
                T, C, D, NE, RD, RANK, KT, TG, NG)
        phase_b(nc, psum, x, Wo, bo, B_T, k_scr, q_scr, z_scr, v_scr, out,
                T, C, D, S, QG, NQ, KEYT, DT)


def phase_a(nc, psum, x, xT, Wqkv, bqkv, b_cols, A_T, WqT, keysT, k_scr, q_scr, z_scr, v_scr, stat_scr,
            T, C, D, NE, RD, RANK, KT, TG, NG):
    NTOK = TG // P
    HALF = TG // W
    IPP = KT // 2
    PRODUCTS = [("feature", lambda r: Wqkv[r, D:2 * D]), ("feature", lambda r: Wqkv[r, 0:D]),
                ("token", lambda r: A_T[r, :]), ("token", lambda r: Wqkv[r, 2 * D:3 * D])]
    IPG = IPP * len(PRODUCTS)
    RAW = 2
    ST = 4
    XS = 4
    M_R = 72
    STAT_STEPS = 5 * NTOK + 4
    GATE_STEPS = 4 * NTOK + 6
    EPS = 1e-5

    def order(product):
        return [*range(1, 8), 0] if product == 2 else [*range(8)]

    with ExitStack() as ctx:
        def sb(name, shape, dt=F32):
            return ctx.enter_context(nc.sbuf_tensor(name, shape, dt))

        def sem(name):
            return ctx.enter_context(nc.semaphore(name))

        x_hi = sb("x_hi", [P, KT, TG], F32R)
        x_lo = sb("x_lo", [P, KT, TG], F32R)
        x_raw = sb("x_raw", [P, XS, TG])
        x_rows = x_raw[:, 2:4, :].rearrange("p a b -> p (a b)")
        w_raw = sb("w_raw", [P, RAW, 2, W])
        w_hi = sb("w_hi", [P, RAW, 2, W], F32R)
        w_lo = sb("w_lo", [P, RAW, 2, W], F32R)
        stage = sb("stage", [P, ST, W])
        mean_rstd = sb("mean_rstd", [P, 2, TG])
        stats = sb("stats", [P, 4, 6])
        mv = sb("mv", [P, 2, NTOK])
        var = sb("var", [P, NTOK])
        std = sb("std", [P, NTOK])
        rs0 = sb("rs0", [P, NTOK])
        rs1 = sb("rs1", [P, NTOK])
        rs2 = sb("rs2", [P, NTOK])
        wq_raw = sb("wq_raw", [P, KT, RD])
        wq = sb("wq", [P, KT, M_R], F32R)
        keys2 = sb("keys2", [2 * RD, NE])
        rq = sb("rq", [2 * RD, TG])
        score = sb("score", [P, NTOK, NE])
        left = sb("left", [P, NTOK, NE])
        left2 = sb("left2", [P, NTOK, NE])
        top = sb("top", [P, NTOK, 8])
        second = sb("second", [P, NTOK, 8])
        gsum = sb("gsum", [P, NTOK])
        b_kq = sb("b_kq", [P, 2, D // P])
        b_v = sb("b_v", [P, D])

        s_const = sem("s_const")
        s_wq = sem("s_wq")
        s_raw = [sem(f"s_raw{i}") for i in range(RAW)]
        s_whi = sem("s_whi")
        s_wlo = sem("s_wlo")
        s_used = sem("s_used")
        s_tile = sem("s_tile")
        s_rq = sem("s_rq")
        s_score = sem("s_score")
        s_evA = sem("s_evA")
        s_evD = sem("s_evD")
        s_out = [sem(f"s_out{i}") for i in range(ST)]
        s_rows = sem("s_rows")
        s_mv = sem("s_mv")
        s_stat = sem("s_stat")
        s_var = sem("s_var")
        s_std = sem("s_std")
        s_rstd = sem("s_rstd")
        s_mst = sem("s_mst")
        s_mld = sem("s_mld")
        s_xraw = [sem(f"s_xraw{i}") for i in range(XS)]
        s_xsub = sem("s_xsub")
        s_xn = sem("s_xn")
        s_xhi = sem("s_xhi")
        s_xlo = sem("s_xlo")
        s_gate = sem("s_gate")
        s_pass = sem("s_pass")
        s_gexp_in = sem("s_gexp_in")
        s_gexp = sem("s_gexp")

        w_rows = [slice(i * 2 * P, (i + 1) * 2 * P) for i in range(IPP)]

        def item(g, it):
            return g * IPG + it

        EVA, EVD = 19, 16

        def taken(engine, g, product, j):
            if product < 2:
                wait(engine, s_evA, g * EVA + (10 if product else 0) + j + 1)
            else:
                wait(engine, s_evD, g * EVD + (8 if product == 3 else 0) + j + 1)

        def tile_ready(engine, g, product, pos):
            if pos < 7:
                engine.wait_ge(s_tile, g * 28 + product * 7 + pos + 1)
            else:
                engine.wait_ge(s_used, item(g, product * IPP + IPP - 1) + 1)

        def loop(engine, body):
            body(0, True)
            with engine.Fori(1, NG - 1) as g:
                body(g, True)
            body(NG - 1, False)

        block = ctx.enter_context(nc.Block())

        @block.sync
        def _(sp):
            sp.dma_start(wq_raw[:], WqT.rearrange("(k p) r -> p k r", p=P)).then_inc(s_const, 16)
            sp.dma_start(keys2[0:RD, :], keysT).then_inc(s_const, 16)
            sp.dma_start(keys2[RD:2 * RD, :], keysT).then_inc(s_const, 16)
            sp.dma_start(b_kq[:, 0, :], b_cols[:, D // P:2 * D // P]).then_inc(s_const, 16)
            sp.dma_start(b_kq[:, 1, :], b_cols[:, 0:D // P]).then_inc(s_const, 16)
            sp.dma_start(b_v[:], bqkv[2 * D:3 * D].rearrange("(a d) -> a d", a=1)
                         .to_broadcast([P, D])).then_inc(s_const, 16)

            def store(g, product):
                for pos, j in enumerate(order(product)):
                    slot = pos % ST
                    taken(sp, g, product, pos)
                    if product < 2:
                        dst = (k_scr, q_scr)[product][(j // HALF) * P:(j // HALF + 1) * P,
                                                      bass.ds(g * TG + (j % HALF) * W, W)]
                    else:
                        dst = (z_scr, v_scr)[product - 2][bass.ds(g * TG + j * P, P), :]
                    sp.dma_start(dst, stage[:, slot, :]).then_inc(s_out[slot], 16)

            def body(g, more):
                for it in range(IPG):
                    n = item(g, it)
                    product, i = it // IPP, it % IPP
                    wait(sp, s_wlo, n - RAW + 1)
                    sp.dma_start(w_raw[:, it % RAW], PRODUCTS[product][1](w_rows[i])
                                 .rearrange("(a p) w -> p a w", p=P)).then_inc(s_raw[it % RAW], 16)
                    if i == 1:
                        if product:
                            store(g, product - 1)
                        elif not (static(g) and g == 0):
                            store(g - 1, len(PRODUCTS) - 1)

            loop(sp, body)
            store(NG - 1, len(PRODUCTS) - 1)
            for slot in range(ST):
                sp.wait_ge(s_out[slot], 16 * NG * IPG // ST)

        def x_pair_load(act, g, pair):
            for k in (2 * pair, 2 * pair + 1):
                act.dma_start(x_raw[:, k % XS, :], xT[k * P:(k + 1) * P, bass.ds(g * TG, TG)]
                              ).then_inc(s_xraw[k % XS], 16)

        def rows_load(act, g, j):
            act.dma_start(x_rows, x[bass.ds(g * TG + j * P, P), :]).then_inc(s_rows, 16)

        @block.scalar
        def _(act):
            def split_weights(g, it):
                n = item(g, it)
                act.wait_ge(s_raw[it % RAW], 16 * (g * (IPG // RAW) + it // RAW + 1))
                wait(act, s_used, n - RAW + 1)
                nc.scalar.activation(w_hi[:, it % RAW], w_raw[:, it % RAW], ACT.Copy).then_inc(s_whi, 1)

            def take_features(g, product):
                for pos, j in enumerate(order(product)):
                    slot = pos % ST
                    tile_ready(act, g, product, pos)
                    wait(act, s_out[slot], 16 * (g * 8 + product * 2 + pos // ST))
                    nc.scalar.activation(stage[:, slot, :], psum[:, j, :], ACT.Identity,
                                         bias=b_kq[:, product, j // HALF:j // HALF + 1]).then_inc(s_evA, 1)

            def split_x_pair(g, pair):
                for k in (2 * pair, 2 * pair + 1):
                    act.wait_ge(s_xn, g * KT + k + 1)
                    wait(act, s_used, item(g - 1, 3 * IPP + pair) + 1)
                    nc.scalar.activation(x_hi[:, k, :], x_raw[:, k % XS, :], ACT.Copy).then_inc(s_xhi, 1)

            def square_roots(g):
                act.wait_ge(s_var, g + 1)
                nc.scalar.activation(std[:], var[:], ACT.Sqrt).then_inc(s_std, 1)

            def store_stats(g):
                act.wait_ge(s_rstd, g + 1)
                for a in range(2):
                    act.dma_start(stat_scr[bass.ds(g, 1), a, :].rearrange("o (j p) -> p (o j)", p=P),
                                  mv[:, a, :], allow_slow_non_contiguous=True).then_inc(s_mst, 16)

            def broadcast_stats(g):
                act.wait_ge(s_mst, 32 * (g + 1))
                act.dma_start(mean_rstd[:].rearrange("p a t -> p (a t)"),
                              stat_scr[bass.ds(g, 1)].rearrange("o a t -> o (a t)")
                              .to_broadcast([P, 2 * TG])).then_inc(s_mld, 16)

            act.wait_ge(s_const, 96)
            act.wait_ge(s_wq, 1)
            nc.scalar.activation(wq[:, :, 0:RD], wq_raw[:], ACT.Copy).then_inc(s_wq, 1)
            for j in range(NTOK):
                wait(act, s_mv, j)
                rows_load(act, 0, j)
            x_pair_load(act, 0, 0)
            square_roots(0)
            store_stats(0)
            x_pair_load(act, 0, 1)
            broadcast_stats(0)

            def body(g, more):
                first = static(g) and g == 0
                for it in range(IPG):
                    product, i = it // IPP, it % IPP
                    split_weights(g, it)
                    if it == IPP:
                        take_features(g, 0)
                        for h in range(HALF):
                            act.wait_ge(s_rq, g * HALF + h + 1)
                            nc.scalar.activation(rq[:, h * W:(h + 1) * W], psum[0:2 * RD, h, :],
                                                 ACT.Copy).then_inc(s_evA, 1)
                    if it == 2 * IPP:
                        take_features(g, 1)
                        act.wait_ge(s_score, g + 1)
                        nc.scalar.activation(score[:].rearrange("p j e -> p (j e)"), psum[:, 0, :],
                                             ACT.Copy).then_inc(s_evA, 1)
                    if it == 2 * IPP + 2:
                        act.wait_ge(s_gexp_in, g + 1)
                        nc.scalar.activation(score[:], score[:], ACT.Exp).then_inc(s_gexp, 1)
                    if first and it < IPP:
                        split_x_pair(0, it)
                        if it + 2 < IPP:
                            act.wait_ge(s_xlo, 2 * it + 2)
                            x_pair_load(act, 0, it + 2)
                    elif it == 0:
                        split_x_pair(g, IPP - 1)
                    if more:
                        if IPP - 1 <= it < IPP - 1 + NTOK:
                            if it == IPP - 1:
                                act.wait_ge(s_xlo, g * KT + KT)
                            else:
                                act.wait_ge(s_mv, (g + 1) * NTOK + it - IPP + 1)
                            rows_load(act, g + 1, it - IPP + 1)
                        if it == 2 * IPP + 1:
                            square_roots(g + 1)
                        if it == 2 * IPP + 3:
                            store_stats(g + 1)
                        if it == 2 * IPP + 4:
                            broadcast_stats(g + 1)
                            x_pair_load(act, g + 1, 0)
                            x_pair_load(act, g + 1, 1)
                        if it > 3 * IPP:
                            pair = it - 3 * IPP - 1
                            split_x_pair(g + 1, pair)
                            if pair + 2 < IPP:
                                act.wait_ge(s_xlo, (g + 1) * KT + 2 * pair + 2)
                                x_pair_load(act, g + 1, pair + 2)

            loop(act, body)

        @block.tensor
        def _(pe):
            def router(g):
                pe.wait_ge(s_wq, 3)
                for h in range(HALF):
                    taken(pe, g, 0, h)
                    for k in range(KT):
                        for part in (x_hi, x_lo):
                            mm = pe.matmul(psum[0:M_R, h, :], wq[:, k, :], part[:, k, h * W:(h + 1) * W],
                                           start=(k == 0 and part is x_hi), stop=(k == KT - 1 and part is x_lo))
                    mm.then_inc(s_rq, 1)

            def scores(g):
                taken(pe, g, 1, 0)
                for j in range(NTOK):
                    mm = pe.matmul(psum[:, 0, j * NE:(j + 1) * NE], rq[:, j * P:(j + 1) * P], keys2[:],
                                   start=True, stop=True)
                mm.then_inc(s_score, 1)

            def bank_free(g, product, pos, j):
                if product == 0:
                    taken(pe, g - 1, 3, pos)
                elif product == 1:
                    if j < HALF:
                        wait(pe, s_evA, g * EVA + 8 + j + 1)
                    else:
                        taken(pe, g, 0, j)
                elif product == 2:
                    if j == 0:
                        wait(pe, s_evA, g * EVA + EVA)
                    else:
                        taken(pe, g, 1, j)
                else:
                    taken(pe, g, 2, order(2).index(j))

            def body(g, more):
                for it in range(IPG):
                    product, i = it // IPP, it % IPP
                    slot = it % RAW
                    pe.wait_ge(s_wlo, item(g, it) + 1)
                    for a in range(2):
                        k = 2 * i + a
                        if product == 0:
                            pe.wait_ge(s_xlo, g * KT + k + 1)
                        for pos, j in enumerate(order(product)):
                            if k == 0:
                                if product == 0 and static(g) and g == 0:
                                    pass
                                else:
                                    bank_free(g, product, pos, j)
                            if PRODUCTS[product][0] == "feature":
                                m, h = j // HALF, j % HALF
                                wh, wl = (w[:, slot, a, m * P:(m + 1) * P] for w in (w_hi, w_lo))
                                xh, xl = (t[:, k, h * W:(h + 1) * W] for t in (x_hi, x_lo))
                                parts = ((wh, xh), (wh, xl), (wl, xh))
                            else:
                                wh, wl = (w[:, slot, a, :] for w in (w_hi, w_lo))
                                xh, xl = (t[:, k, j * P:(j + 1) * P] for t in (x_hi, x_lo))
                                parts = ((xh, wh), (xh, wl), (xl, wh))
                            for n, (stationary, moving) in enumerate(parts):
                                mm = pe.matmul(psum[:, j, :], stationary, moving,
                                               start=(k == 0 and n == 0), stop=(k == KT - 1 and n == 2))
                            if k == KT - 1 and pos < 7:
                                mm.then_inc(s_tile, 1)
                    mm.then_inc(s_used, 1)
                    if it == IPP - 1:
                        router(g)
                    if it == 2 * IPP - 1:
                        scores(g)

            loop(pe, body)

        @block.vector
        def _(dve):
            def split_weights(g, it):
                n = item(g, it)
                dve.wait_ge(s_whi, n + 1)
                nc.vector.tensor_tensor(w_lo[:, it % RAW], w_raw[:, it % RAW],
                                        w_hi[:, it % RAW].bitcast(F32), ALU.subtract).then_inc(s_wlo, 1)

            def take_tokens(g, product):
                for pos, j in enumerate(order(product)):
                    slot = pos % ST
                    tile_ready(dve, g, product, pos)
                    wait(dve, s_out[slot], 16 * (g * 8 + product * 2 + pos // ST))
                    if product == 2:
                        ins = nc.vector.tensor_tensor(
                            stage[:, slot, :].rearrange("p (e r) -> p e r", r=RANK),
                            psum[:, j, :].rearrange("p (e r) -> p e r", r=RANK),
                            score[:, j, :].unsqueeze(2).to_broadcast([P, NE, RANK]), ALU.mult)
                    else:
                        ins = nc.vector.tensor_tensor(stage[:, slot, :], psum[:, j, :], b_v[:], ALU.add)
                    ins.then_inc(s_evD, 1)

            def normalise_pair(g, pair):
                ks = (2 * pair, 2 * pair + 1)
                wait(dve, s_mld, 16 * (g + 1))
                for k in ks:
                    dve.wait_ge(s_xraw[k % XS], 16 * (g * (KT // XS) + k // XS + 1))
                    nc.vector.tensor_tensor(x_raw[:, k % XS, :], x_raw[:, k % XS, :], mean_rstd[:, 0, :],
                                            ALU.subtract).then_inc(s_xsub, 1)
                for k in ks:
                    dve.wait_ge(s_xsub, g * KT + k + 1)
                    nc.vector.tensor_tensor(x_raw[:, k % XS, :], x_raw[:, k % XS, :], mean_rstd[:, 1, :],
                                            ALU.mult).then_inc(s_xn, 1)
                for k in ks:
                    dve.wait_ge(s_xhi, g * KT + k + 1)
                    nc.vector.tensor_tensor(x_lo[:, k, :], x_raw[:, k % XS, :], x_hi[:, k, :].bitcast(F32),
                                            ALU.subtract).then_inc(s_xlo, 1)

            def stats_of_tile(g, j):
                chain = Chain(dve, s_stat, g * STAT_STEPS + 5 * j)
                dve.wait_ge(s_rows, 16 * (g * NTOK + j + 1))
                for c in range(4):
                    chain.step(nc.vector.bn_stats(stats[:, c, :], x_rows[:, c * W:(c + 1) * W]))
                chain.wait()
                dve.sem_inc(s_pass, 1)
                chain.link(nc.vector.bn_aggr(mv[:, :, j], stats[:].rearrange("p a b -> p (a b)")))
                nc.vector.tensor_copy(var[:, j:j + 1], mv[:, 1, j:j + 1]).then_inc(s_mv, 1)

            def rstd_ready(g):
                dve.wait_ge(s_mv, (g + 1) * NTOK)
                nc.vector.tensor_scalar(var[:], var[:], EPS, None, ALU.add).then_inc(s_var, 1)

            def rstd_finish(g):
                chain = Chain(dve, s_stat, g * STAT_STEPS + 5 * NTOK)
                dve.wait_ge(s_std, g + 1)
                chain.link(nc.vector.reciprocal(rs0[:], std[:]))
                chain.link(nc.vector.tensor_tensor(rs1[:], rs0[:], rs0[:], ALU.mult))
                chain.link(nc.vector.tensor_tensor(rs2[:], rs1[:], var[:], ALU.mult))
                chain.link(nc.vector.tensor_scalar(rs1[:], rs2[:], -0.5, 1.5, ALU.mult, ALU.add))
                nc.vector.tensor_tensor(mv[:, 1, :], rs0[:], rs1[:], ALU.mult).then_inc(s_rstd, 1)

            def pick_experts(g):
                chain = Chain(dve, s_gate, g * GATE_STEPS)
                dve.wait_ge(s_evA, g * EVA + EVA)
                dve.sem_inc(s_pass, 1)
                for j in range(NTOK):
                    chain.step(nc.vector.max(top[:, j, :], score[:, j, :]))
                for j in range(NTOK):
                    chain.wait(NTOK - 1)
                    dve.sem_inc(s_pass, 1)
                    chain.step(nc.vector.match_replace(left[:, j, :], top[:, j, :], score[:, j, :], LOWEST))
                for j in range(NTOK):
                    chain.wait(NTOK - 1)
                    dve.sem_inc(s_pass, 1)
                    chain.step(nc.vector.max(second[:, j, :], left[:, j, :]))
                for j in range(NTOK):
                    chain.wait(NTOK - 1)
                    dve.sem_inc(s_pass, 1)
                    chain.step(nc.vector.match_replace(left2[:, j, :], second[:, j, :], left[:, j, :], LOWEST))
                chain.wait()
                chain.link(nc.vector.tensor_tensor(left[:], left2[:], score[:], ALU.not_equal))
                nc.vector.tensor_tensor(score[:], score[:], top[:, :, 0:1].to_broadcast([P, NTOK, NE]),
                                        ALU.subtract).then_inc(s_gexp_in, 1)

            def finish_gates(g):
                chain = Chain(dve, s_gate, g * GATE_STEPS + 4 * NTOK + 1)
                dve.wait_ge(s_gexp, g + 1)
                chain.link(nc.vector.tensor_tensor(score[:], score[:], left[:], ALU.mult))
                chain.link(nc.vector.tensor_reduce(gsum[:], score[:], AX.X, ALU.add))
                chain.link(nc.vector.tensor_scalar(gsum[:], gsum[:], 0.5, None, ALU.mult))
                chain.link(nc.vector.reciprocal(gsum[:], gsum[:]))
                chain.link(nc.vector.tensor_tensor(score[:], score[:], gsum[:].unsqueeze(2)
                                                   .to_broadcast([P, NTOK, NE]), ALU.mult))

            nc.vector.memset(wq[:].bitcast(F32), 0.0).then_inc(s_wq, 1)
            dve.wait_ge(s_wq, 2)
            nc.vector.tensor_tensor(wq[:, :, RD:2 * RD], wq_raw[:], wq[:, :, 0:RD].bitcast(F32),
                                    ALU.subtract).then_inc(s_wq, 1)
            for j in range(NTOK):
                stats_of_tile(0, j)
            rstd_ready(0)
            rstd_finish(0)

            def body(g, more):
                first = static(g) and g == 0
                for it in range(IPG):
                    split_weights(g, it)
                    if it == 0 and not first:
                        take_tokens(g - 1, 3)
                    if it == 3 * IPP:
                        take_tokens(g, 2)
                    if first and it < IPP:
                        normalise_pair(0, it)
                    elif it == 0:
                        normalise_pair(g, IPP - 1)
                    if it == 2 * IPP:
                        pick_experts(g)
                    if it == 2 * IPP + 4:
                        finish_gates(g)
                    if more:
                        if IPP <= it < IPP + NTOK:
                            stats_of_tile(g + 1, it - IPP)
                        if it == 2 * IPP + 1:
                            rstd_ready(g + 1)
                        if it == 2 * IPP + 2:
                            rstd_finish(g + 1)
                        if it > 3 * IPP:
                            normalise_pair(g + 1, it - 3 * IPP - 1)

            loop(dve, body)
            take_tokens(NG - 1, 3)


def phase_b(nc, psum, x, Wo, bo, B_T, k_scr, q_scr, z_scr, v_scr, out, T, C, D, S, QG, NQ, KEYT, DT):
    RING = 4
    S_IT, O_IT, V_IT = KEYT // 2, 16, KEYT // 2
    PER = S_IT + O_IT + V_IT
    CB = C // W
    OPB = O_IT // CB
    QT = QG // P
    PR = 4
    XO = 8
    MISC = 7
    SCALE = float(D) ** -0.5
    S_BANK = [i % 7 for i in range(KEYT)]
    O_BANK = [i % 7 for i in range(CB * QT)]
    V_BANK = [2, 3, 4, 5]
    V_AFTER = [max(i for i, b in enumerate(O_BANK) if b == v) for v in V_BANK]
    S_LAST = [max(i for i, b in enumerate(S_BANK) if b == v) for v in range(7)]
    MAX_STEPS = KEYT - 1
    TOP_STEPS = 1

    with ExitStack() as ctx:
        def sb(name, shape, dt=F32):
            return ctx.enter_context(nc.sbuf_tensor(name, shape, dt))

        def sem(name):
            return ctx.enter_context(nc.semaphore(name))

        r_raw = sb("r_raw", [P, RING, 2 * W])
        r_hi = sb("r_hi", [P, RING, 2 * W], F32R)
        r_lo = sb("r_lo", [P, RING, 2 * W], F32R)
        prob = sb("prob", [P, KEYT, QG])
        p_hi = sb("p_hi", [P, PR, QG], F32R)
        p_lo = sb("p_lo", [P, PR, QG], F32R)
        q_raw = sb("q_raw", [P, DT, QG])
        q_hi = sb("q_hi", [P, DT, QG], F32R)
        q_lo = sb("q_lo", [P, DT, QG], F32R)
        z_raw = sb("z_raw", [P, QT, D])
        f_hi = sb("f_hi", [P, 2 * DT, QG], F32R)
        f_lo = sb("f_lo", [P, 2 * DT, QG], F32R)
        attn = sb("attn", [P, DT, QG])
        res = sb("res", [P, XO, W])
        b_out = sb("b_out", [P, C])
        ident = sb("ident", [P, P])
        ones = sb("ones", [P, P])
        run_max = sb("run_max", [P, QG])
        q_max = sb("q_max", [P, QT])
        diag = sb("diag", [P, QT, P])
        max_all = sb("max_all", [P, QG])
        run_sum = sb("run_sum", [P, QG])
        inv_sum = sb("inv_sum", [P, QG])

        b_const = sem("b_const")
        b_ones = sem("b_ones")
        b_raw = [sem(f"b_raw{i}") for i in range(RING)]
        b_hi = sem("b_hi")
        b_lo = sem("b_lo")
        b_used = sem("b_used")
        b_q = sem("b_q")
        b_qhi = sem("b_qhi")
        b_qlo = sem("b_qlo")
        b_s = sem("b_s")
        b_copy = sem("b_copy")
        b_max = sem("b_max")
        b_tr = sem("b_tr")
        b_qmax = sem("b_qmax")
        b_diag = sem("b_diag")
        b_bc = sem("b_bc")
        b_mall = sem("b_mall")
        b_sub = sem("b_sub")
        b_exp = sem("b_exp")
        b_acc = sem("b_acc")
        b_sum = sem("b_sum")
        b_inv = sem("b_inv")
        b_phi = sem("b_phi")
        b_plo = sem("b_plo")
        b_pused = sem("b_pused")
        b_pv = sem("b_pv")
        b_attn = sem("b_attn")
        b_ahi = sem("b_ahi")
        b_alo = sem("b_alo")
        b_z = sem("b_z")
        b_zt = sem("b_zt")
        b_zhi = sem("b_zhi")
        b_zlo = sem("b_zlo")
        b_o = sem("b_o")
        b_oev = sem("b_oev")
        b_x = [sem(f"b_x{i}") for i in range(XO)]
        b_xb = sem("b_xb")
        b_st = [sem(f"b_st{i}") for i in range(XO)]

        def number(t, it):
            if static(t) and t == 0 and it < S_IT:
                return it
            if static(t) and t == NQ:
                return PER * NQ - O_IT + it - S_IT
            return PER * t - O_IT + it

        def uses(t, it):
            n = number(t, it)
            if static(n):
                return n // RING + 1
            return t * (PER // RING) + (it - O_IT) // RING + 1

        def segments(engine, scores, output, values):
            scores(0)
            values(0, True)
            scores(1)
            output(0, True)
            values(1, True)
            with engine.Fori(2, NQ - 1) as t:
                scores(t)
                output(t - 1, True)
                values(t, True)
            scores(NQ - 1)
            output(NQ - 2, True)
            values(NQ - 1, False)

        def score_ready(engine, t, i):
            if i % 2 == 0:
                engine.wait_ge(b_s, t * (KEYT // 2) + i // 2 + 1)
            else:
                engine.wait_ge(b_used, number(t, i // 2) + 1)

        def out_ready(engine, u, c, j):
            if j < QT - 1:
                engine.wait_ge(b_o, u * CB * (QT - 1) + c * (QT - 1) + j + 1)
            else:
                engine.wait_ge(b_used, number(u + 1, S_IT + c * OPB + OPB - 1) + 1)

        block = ctx.enter_context(nc.Block())

        @block.sync
        def _(sp):
            def fetch(t, it, source):
                slot = it % RING
                wait(sp, b_lo, number(t, it) - RING + 1)
                sp.dma_start(r_raw[:, slot, :].rearrange("p (a w) -> p a w", a=source.shape[1]),
                             source).then_inc(b_raw[slot], 16)

            def queries(t):
                sp.dma_start(q_raw[:], q_scr.rearrange("(m p) t -> p m t", p=P)[:, :, bass.ds(t * QG, QG)]
                             ).then_inc(b_q, 16)

            def batch_base(t):
                return (t // (NQ * QG // T * (S // QG))) * S if static(t) else (t // (S // QG)) * S

            def store_block(u, c):
                for j in range(QT):
                    slot = (c * QT + j) % XO
                    sp.wait_ge(b_oev, u * CB * QT + c * QT + j + 1)
                    sp.dma_start(out[bass.ds(u * QG + j * P, P), c * W:(c + 1) * W], res[:, slot, :]
                                 ).then_inc(b_st[slot], 16)

            def load_block(u, c):
                for j in range(QT):
                    slot = (c * QT + j) % XO
                    wait(sp, b_st[slot], 16 * (u * (CB * QT // XO) + (c * QT + j) // XO))
                    sp.dma_start(res[:, slot, :], x[bass.ds(u * QG + j * P, P), c * W:(c + 1) * W]
                                 ).then_inc(b_x[slot], 16)

            def scores(t):
                base = batch_base(t)
                for i in range(S_IT):
                    fetch(t, i, k_scr.rearrange("(m p) t -> p m t", p=P)[:, :, bass.ds(base + i * 2 * P, 2 * P)])

            def output(u, softmax):
                for i in range(O_IT):
                    c, part = i // OPB, i % OPB
                    source, row = (B_T, part * 2 * P) if part < OPB // 2 else (Wo, (part - OPB // 2) * 2 * P)
                    fetch(u + 1, S_IT + i, source[row:row + 2 * P, c * W:(c + 1) * W]
                          .rearrange("(a p) w -> p a w", p=P))
                    if part == 0 and c >= 2:
                        store_block(u, c - 2)
                    if part == 1:
                        load_block(u, c)

            def values(t, more):
                base = batch_base(t)
                for i in range(V_IT):
                    fetch(t, S_IT + O_IT + i, v_scr[bass.ds(base + i * 2 * P, 2 * P), :]
                          .rearrange("(a p) w -> p a w", p=P))
                    if i == 0:
                        wait(sp, b_zt, QT * t)
                        sp.dma_start(z_raw[:], z_scr[bass.ds(t * QG, QG), :]
                                     .rearrange("(a p) w -> p a w", p=P)).then_inc(b_z, 16)
                        if more:
                            wait(sp, b_qlo, 2 * (t + 1))
                            queries(t + 1)
                    if not (static(t) and t == 0):
                        if i == 0:
                            store_block(t - 1, CB - 2)
                        if i == 4:
                            store_block(t - 1, CB - 1)

            sp.dma_start(b_out[:], bo.rearrange("(a d) -> a d", a=1).to_broadcast([P, C])).then_inc(b_const, 16)
            queries(0)
            segments(sp, scores, output, values)
            output(NQ - 1, False)
            store_block(NQ - 1, CB - 2)
            store_block(NQ - 1, CB - 1)
            for slot in range(XO):
                sp.wait_ge(b_st[slot], 16 * NQ * CB * QT // XO)

        @block.scalar
        def _(act):
            def split(t, it):
                slot, n = it % RING, number(t, it)
                act.wait_ge(b_raw[slot], 16 * uses(t, it))
                wait(act, b_used, n - RING + 1)
                nc.scalar.activation(r_hi[:, slot, :], r_raw[:, slot, :], ACT.Copy).then_inc(b_hi, 1)

            def split_queries(t, half):
                act.wait_ge(b_q, 16 * (t + 1))
                wait(act, b_used, number(t - 1, S_IT - 1) + 1 if not (static(t) and t == 0) else 0)
                rows = slice(half * DT // 2, (half + 1) * DT // 2)
                nc.scalar.activation(q_hi[:, rows, :], q_raw[:, rows, :], ACT.Copy).then_inc(b_qhi, 1)

            def take_scores(t, i):
                score_ready(act, t, i)
                wait(act, b_plo, (t - 1) * KEYT + i + 1)
                wait(act, b_acc, t * (KEYT - 1))
                nc.scalar.activation(prob[:, i, :], psum[:, S_BANK[i], :], ACT.Copy).then_inc(b_copy, 1)

            def take_maximum(t):
                act.wait_ge(b_bc, t + 1)
                nc.scalar.activation(max_all[:], psum[:, MISC, :], ACT.Copy).then_inc(b_mall, 1)

            def exponential(t, i):
                act.wait_ge(b_sub, t * KEYT + i + 1)
                nc.scalar.activation(prob[:, i, :], prob[:, i, :], ACT.Exp, scale=SCALE).then_inc(b_exp, 1)

            def split_attention(t):
                for d in range(DT):
                    act.wait_ge(b_attn, t * DT + d + 1)
                    nc.scalar.activation(f_hi[:, d, :], attn[:, d, :], ACT.Copy).then_inc(b_ahi, 1)

            def split_z(t, m):
                act.wait_ge(b_zt, t * DT + m + 1)
                nc.scalar.activation(f_hi[:, DT + m, :], psum[:, MISC, :], ACT.Copy).then_inc(b_zhi, 1)

            def finish_values(t):
                split_z(t, DT - 1)
                split_attention(t)

            def scores(t):
                for i in range(S_IT):
                    split(t, i)
                    if i == 0 and not (static(t) and t == 0):
                        finish_values(t - 1)
                    if i >= 1:
                        take_scores(t, 2 * i - 2)
                        take_scores(t, 2 * i - 1)

            def softmax_step(t, i):
                if i == 0:
                    take_scores(t, KEYT - 2)
                    take_scores(t, KEYT - 1)
                if i == 3:
                    take_maximum(t)
                if 4 <= i < 12:
                    exponential(t, 2 * i - 8)
                    exponential(t, 2 * i - 7)

            def output(u, softmax):
                for i in range(O_IT):
                    split(u + 1, S_IT + i)
                    if softmax:
                        softmax_step(u + 1, i)

            def values(t, more):
                if static(t) and t == 0:
                    for i in range(O_IT):
                        softmax_step(t, i)
                for i in range(V_IT):
                    split(t, S_IT + O_IT + i)
                    for k in (2 * i, 2 * i + 1):
                        if k >= PR:
                            if k % 2 == 0:
                                act.wait_ge(b_pused, t * (KEYT // 2) + (k - PR) // 2 + 1)
                            else:
                                act.wait_ge(b_used, number(t, S_IT + O_IT + (k - PR) // 2) + 1)
                        act.wait_ge(b_exp, t * KEYT + k + 1)
                        nc.scalar.activation(p_hi[:, k % PR, :], prob[:, k, :], ACT.Copy).then_inc(b_phi, 1)
                    if i >= 5:
                        split_z(t, i - 5)
                    if more and i in (5, 6):
                        split_queries(t + 1, i - 5)

            split_queries(0, 0)
            split_queries(0, 1)
            segments(act, scores, output, values)
            finish_values(NQ - 1)
            output(NQ - 1, False)

        @block.tensor
        def _(pe):
            def three(bank, sh, sl, mh, ml, first, last):
                pe.matmul(bank, sh, mh, start=first, stop=False)
                pe.matmul(bank, sh, ml, start=False, stop=False)
                return pe.matmul(bank, sl, mh, start=False, stop=last)

            def streamed(t, it):
                pe.wait_ge(b_lo, number(t, it) + 1)
                return r_hi[:, it % RING, :], r_lo[:, it % RING, :]

            def scores(t):
                pe.wait_ge(b_qlo, 2 * (t + 1))
                for i in range(S_IT):
                    kh, kl = streamed(t, i)
                    for a in range(2):
                        tile = 2 * i + a
                        bank = S_BANK[tile]
                        if tile >= 7:
                            pe.wait_ge(b_copy, t * KEYT + tile - 7 + 1)
                        elif not (static(t) and t == 0):
                            if bank in V_BANK:
                                pe.wait_ge(b_attn, (t - 1) * DT + V_BANK.index(bank) + 1)
                            else:
                                wait(pe, b_oev, (t - 1) * CB * QT)
                        for d in range(DT):
                            cols = slice(d * 2 * P + a * P, d * 2 * P + (a + 1) * P)
                            mm = three(psum[:, bank, :], kh[:, cols], kl[:, cols],
                                       q_hi[:, d, :], q_lo[:, d, :], d == 0, d == DT - 1)
                        mm.then_inc((b_s, b_used)[a], 1)

            def transpose_maxima(t):
                pe.wait_ge(b_max, (t + 1) * MAX_STEPS)
                wait(pe, b_zlo, t * DT)
                for j in range(QT):
                    mm = pe.transpose(psum[:, MISC, j * P:(j + 1) * P], run_max[:, j * P:(j + 1) * P], ident[:])
                mm.then_inc(b_tr, 1)

            def broadcast_maxima(t):
                pe.wait_ge(b_diag, (t + 1) * QT)
                for j in range(QT):
                    mm = pe.matmul(psum[:, MISC, j * P:(j + 1) * P], ones[:], diag[:, j, :], start=True, stop=True)
                mm.then_inc(b_bc, 1)

            def total(t):
                pe.wait_ge(b_acc, (t + 1) * (KEYT - 1))
                pe.matmul(psum[:, MISC, :], ones[:], run_sum[:], start=True, stop=True).then_inc(b_sum, 1)

            def output(u, softmax):
                for c in range(CB):
                    for part in range(OPB):
                        i = c * OPB + part
                        wh, wl = streamed(u + 1, S_IT + i)
                        first = OPB // 2 <= part
                        f0 = (part - OPB // 2) * 2 if first else DT + 2 * part
                        if i == 0:
                            pe.wait_ge(b_zlo, (u + 1) * DT)
                        if i == OPB // 2:
                            pe.wait_ge(b_alo, (u + 1) * DT)
                        for a in range(2):
                            for j in range(QT):
                                tile = c * QT + j
                                bank = O_BANK[tile]
                                if part == 0 and a == 0:
                                    if tile >= 7:
                                        pe.wait_ge(b_oev, u * CB * QT + tile - 7 + 1)
                                    elif softmax:
                                        pe.wait_ge(b_copy, (u + 1) * KEYT + S_LAST[bank] + 1)
                                    else:
                                        pe.wait_ge(b_attn, (u + 1) * DT)
                                        pe.wait_ge(b_oev, u * CB * QT)
                                tok = slice(j * P, (j + 1) * P)
                                cols = slice(a * W, (a + 1) * W)
                                mm = three(psum[:, bank, :], f_hi[:, f0 + a, tok], f_lo[:, f0 + a, tok],
                                           wh[:, cols], wl[:, cols], part == 0 and a == 0,
                                           part == OPB - 1 and a == 1)
                                if part == OPB - 1 and a == 1 and j < QT - 1:
                                    mm.then_inc(b_o, 1)
                        mm.then_inc(b_used, 1)
                        if softmax and i == 0:
                            transpose_maxima(u + 1)
                        if softmax and i == 2:
                            broadcast_maxima(u + 1)

            def values(t, more):
                if static(t) and t == 0:
                    transpose_maxima(t)
                    broadcast_maxima(t)
                for i in range(V_IT):
                    vh, vl = streamed(t, S_IT + O_IT + i)
                    for a in range(2):
                        k = 2 * i + a
                        pe.wait_ge(b_plo, t * KEYT + k + 1)
                        for d in range(DT):
                            bank = V_BANK[d]
                            if k == 0:
                                if static(t) and t == 0:
                                    pe.wait_ge(b_copy, S_LAST[bank] + 1)
                                else:
                                    pe.wait_ge(b_oev, (t - 1) * CB * QT + V_AFTER[d] + 1)
                            cols = slice(a * W + d * P, a * W + (d + 1) * P)
                            mm = three(psum[:, bank, :], vh[:, cols], vl[:, cols], p_hi[:, k % PR, :],
                                       p_lo[:, k % PR, :], k == 0, k == KEYT - 1)
                            if k == KEYT - 1 and d < DT - 1:
                                mm.then_inc(b_pv, 1)
                        if a == 0:
                            mm.then_inc(b_pused, 1)
                    mm.then_inc(b_used, 1)
                    if i == 3:
                        total(t)
                    if i >= 4:
                        m = i - 4
                        if m == 0:
                            pe.wait_ge(b_z, 16 * (t + 1))
                            pe.wait_ge(b_inv, t + 1)
                        else:
                            pe.wait_ge(b_zlo, t * DT + m)
                        for j in range(QT):
                            mm = pe.transpose(psum[:, MISC, j * P:(j + 1) * P],
                                              z_raw[:, j, m * P:(m + 1) * P], ident[:])
                        mm.then_inc(b_zt, 1)

            pe.wait_ge(b_ones, 2)
            segments(pe, scores, output, values)
            output(NQ - 1, False)

        @block.gpsimd
        def _(pool):
            pool.wait_ge(b_ones, 1)
            nc.gpsimd.affine_select(out=ident[:], in_=ident[:], compare_op=ALU.not_equal, fill=1.0, base=0,
                                    pattern=[[-1, P]], channel_multiplier=1).then_inc(b_ones, 1)
            pool.wait_ge(b_const, 16)

            def add_bias(u, c):
                for j in range(QT):
                    slot = (c * QT + j) % XO
                    pool.wait_ge(b_x[slot], 16 * (u * (CB * QT // XO) + (c * QT + j) // XO + 1))
                    nc.gpsimd.tensor_tensor(res[:, slot, :], res[:, slot, :], b_out[:, c * W:(c + 1) * W],
                                            ALU.add).then_inc(b_xb, 1)

            def sums(t, tiles):
                for i in tiles:
                    pool.wait_ge(b_exp, t * KEYT + i + 1)
                    if i == 1:
                        wait(pool, b_sum, t)
                        nc.gpsimd.tensor_tensor(run_sum[:], prob[:, 0, :], prob[:, 1, :], ALU.add).then_inc(b_acc, 1)
                    else:
                        pool.wait_ge(b_acc, t * (KEYT - 1) + i - 1)
                        nc.gpsimd.tensor_tensor(run_sum[:], run_sum[:], prob[:, i, :], ALU.add).then_inc(b_acc, 1)

            def scores(t):
                pass

            def output(u, softmax):
                for c in range(CB):
                    add_bias(u, c)
                    if softmax and c < 3:
                        sums(u + 1, (range(1, 6), range(6, 12), range(12, KEYT))[c])

            def values(t, more):
                if static(t) and t == 0:
                    sums(t, range(1, KEYT))

            segments(pool, scores, output, values)
            output(NQ - 1, False)

        @block.vector
        def _(dve):
            def split(t, it):
                slot = it % RING
                dve.wait_ge(b_hi, number(t, it) + 1)
                nc.vector.tensor_tensor(r_lo[:, slot, :], r_raw[:, slot, :], r_hi[:, slot, :].bitcast(F32),
                                        ALU.subtract).then_inc(b_lo, 1)

            def split_queries(t, half):
                dve.wait_ge(b_qhi, 2 * t + half + 1)
                rows = slice(half * DT // 2, (half + 1) * DT // 2)
                nc.vector.tensor_tensor(q_lo[:, rows, :], q_raw[:, rows, :], q_hi[:, rows, :].bitcast(F32),
                                        ALU.subtract).then_inc(b_qlo, 1)

            def maximum(t, i):
                dve.wait_ge(b_copy, t * KEYT + i + 1)
                if i == 1:
                    nc.vector.tensor_tensor(run_max[:], prob[:, 0, :], prob[:, 1, :], ALU.max).then_inc(b_max, 1)
                elif i > 1:
                    dve.wait_ge(b_max, t * MAX_STEPS + i - 1)
                    nc.vector.tensor_tensor(run_max[:], run_max[:], prob[:, i, :], ALU.max).then_inc(b_max, 1)

            def query_maxima(t):
                dve.wait_ge(b_tr, t + 1)
                nc.vector.tensor_reduce(q_max[:], psum[:, MISC, :].rearrange("p (j k) -> p j k", j=QT), AX.X,
                                        ALU.max).then_inc(b_qmax, 1)
                dve.wait_ge(b_qmax, t + 1)
                for j in range(QT):
                    nc.vector.tensor_scalar(diag[:, j, :], ident[:], q_max[:, j:j + 1], None,
                                            ALU.mult).then_inc(b_diag, 1)

            def less_maximum(t, i):
                dve.wait_ge(b_mall, t + 1)
                nc.vector.tensor_tensor(prob[:, i, :], prob[:, i, :], max_all[:], ALU.subtract).then_inc(b_sub, 1)

            def softmax_step(t, i):
                if i == 0:
                    maximum(t, KEYT - 2)
                    maximum(t, KEYT - 1)
                if i == 1:
                    query_maxima(t)
                if 4 <= i < 12:
                    less_maximum(t, 2 * i - 8)
                    less_maximum(t, 2 * i - 7)

            def take_attention(t):
                for d in range(DT):
                    if d < DT - 1:
                        dve.wait_ge(b_pv, t * (DT - 1) + d + 1)
                    else:
                        dve.wait_ge(b_used, number(t, PER - 1) + 1)
                    dve.wait_ge(b_inv, t + 1)
                    nc.vector.tensor_tensor(attn[:, d, :], psum[:, V_BANK[d], :], inv_sum[:],
                                            ALU.mult).then_inc(b_attn, 1)
                for d in range(DT):
                    dve.wait_ge(b_ahi, t * DT + d + 1)
                    nc.vector.tensor_tensor(f_lo[:, d, :], attn[:, d, :], f_hi[:, d, :].bitcast(F32),
                                            ALU.subtract).then_inc(b_alo, 1)

            def split_z(t, m):
                dve.wait_ge(b_zhi, t * DT + m + 1)
                nc.vector.tensor_tensor(f_lo[:, DT + m, :], psum[:, MISC, :], f_hi[:, DT + m, :].bitcast(F32),
                                        ALU.subtract).then_inc(b_zlo, 1)

            def finish_values(t):
                split_z(t, DT - 1)
                take_attention(t)

            def take_output(u, c):
                for j in range(QT):
                    tile = c * QT + j
                    out_ready(dve, u, c, j)
                    dve.wait_ge(b_xb, u * CB * QT + tile + 1)
                    nc.vector.tensor_tensor(res[:, tile % XO, :], psum[:, O_BANK[tile], :], res[:, tile % XO, :],
                                            ALU.add).then_inc(b_oev, 1)

            def scores(t):
                for i in range(S_IT):
                    split(t, i)
                    if i == 0 and not (static(t) and t == 0):
                        finish_values(t - 1)
                    if i >= 1:
                        maximum(t, 2 * i - 2)
                        maximum(t, 2 * i - 1)

            def output(u, softmax):
                for i in range(O_IT):
                    split(u + 1, S_IT + i)
                    if i and i % OPB == 0:
                        take_output(u, i // OPB - 1)
                    if softmax:
                        softmax_step(u + 1, i)

            def values(t, more):
                if static(t) and t == 0:
                    for i in range(O_IT):
                        softmax_step(t, i)
                for i in range(V_IT):
                    split(t, S_IT + O_IT + i)
                    for k in (2 * i, 2 * i + 1):
                        dve.wait_ge(b_phi, t * KEYT + k + 1)
                        nc.vector.tensor_tensor(p_lo[:, k % PR, :], prob[:, k, :], p_hi[:, k % PR, :].bitcast(F32),
                                                ALU.subtract).then_inc(b_plo, 1)
                    if i == 0 and not (static(t) and t == 0):
                        take_output(t - 1, CB - 1)
                    if i == 4:
                        dve.wait_ge(b_sum, t + 1)
                        nc.vector.reciprocal(inv_sum[:], psum[:, MISC, :]).then_inc(b_inv, 1)
                    if i >= 5:
                        split_z(t, i - 5)
                    if more and i in (5, 6):
                        split_queries(t + 1, i - 5)

            nc.vector.memset(ones[:], 1.0)
            nc.vector.memset(ident[:], 0.0).then_inc(b_ones, 1)
            split_queries(0, 0)
            split_queries(0, 1)
            segments(dve, scores, output, values)
            finish_values(NQ - 1)
            output(NQ - 1, False)
            take_output(NQ - 1, CB - 1)


def kernel(L0_attn_x, L0_attn_Wqkv, L0_attn_bqkv, L0_attn_Wo, L0_attn_bo, L0_ffn_A_w, L0_ffn_B_w,
           L0_ffn_Wq_w, L0_ffn_keys):
    import numpy as np
    import concourse.bacc as bacc
    from concourse.bass_utils import run_bass_kernel_spmd

    B, S, C = L0_attn_x.shape
    x = np.ascontiguousarray(L0_attn_x).reshape(B * S, C)
    arrays = {
        "x": x,
        "xT": np.ascontiguousarray(x.T),
        "Wqkv": np.ascontiguousarray(L0_attn_Wqkv),
        "bqkv": np.ascontiguousarray(L0_attn_bqkv),
        "b_cols": np.ascontiguousarray(np.reshape(L0_attn_bqkv, (-1, P)).T),
        "Wo": np.ascontiguousarray(L0_attn_Wo),
        "bo": np.ascontiguousarray(L0_attn_bo),
        "A_T": np.ascontiguousarray(np.transpose(L0_ffn_A_w)),
        "B_T": np.ascontiguousarray(np.transpose(L0_ffn_B_w)),
        "WqT": np.ascontiguousarray(np.transpose(L0_ffn_Wq_w)),
        "keysT": np.ascontiguousarray(np.transpose(L0_ffn_keys)),
    }
    nc = bacc.Bacc("TRN2", target_bir_lowering=False, num_devices=1)
    args = [nc.dram_tensor(name, a.shape, mybir.dt.from_np(a.dtype), kind="ExternalInput").ap()
            for name, a in arrays.items()]
    out = nc.dram_tensor("out", [B * S, C], F32, kind="ExternalOutput").ap()
    layer_kernel(nc, *args, out)
    r = run_bass_kernel_spmd(nc, [arrays], core_ids=[0])
    return r.results[0]["out"].reshape(B, S, C)
```

```python
from contextlib import ExitStack

import concourse.bass as bass
from concourse import mybir

ALU = mybir.AluOpType
ACT = mybir.ActivationFunctionType
F32 = mybir.dt.float32
F32R = mybir.dt.float32r
AX = mybir.AxisListType

P = 128
BANKS = 8
W = 512
X_KEPT = 12
LOWEST = -3.0e38


def static(v):
    return isinstance(v, int)


def wait(engine, sem, value):
    if static(value) and value <= 0:
        return
    engine.wait_ge(sem, value)


class Chain:

    def __init__(self, engine, sem, base):
        self.engine, self.sem, self.base, self.n = engine, sem, base, 0

    def step(self, instruction):
        self.n += 1
        instruction.then_inc(self.sem, 1)

    def wait(self, back=0):
        self.engine.wait_ge(self.sem, self.base + self.n - back)

    def link(self, instruction):
        self.step(instruction)
        self.wait()


def layer_kernel(nc, x, xT, Wqkv, bqkv, b_cols, Wo, bo, A_T, B_T, WqT, keysT, out):
    T, C = x.shape
    D = Wo.shape[0]
    NE, RD = keysT.shape[1], keysT.shape[0]
    RANK = D // NE
    NB = 2
    S = T // NB
    KT = C // P
    TG = 1024
    NG = T // TG
    QG = 512
    NQ = T // QG
    KEYT = S // P
    DT = D // P
    assert D == W and KT == 16 and KEYT == 16 and DT == 4 and A_T.shape[1] == D

    k_scr = nc.dram_tensor("k_scratch", [D, T], F32, kind="Internal").ap()
    q_scr = nc.dram_tensor("q_scratch", [D, T], F32, kind="Internal").ap()
    z_scr = nc.dram_tensor("z_scratch", [T, D], F32, kind="Internal").ap()
    v_scr = nc.dram_tensor("v_scratch", [T, D], F32, kind="Internal").ap()
    stat_scr = nc.dram_tensor("stat_scratch", [NG, 2, TG], F32, kind="Internal").ap()

    with ExitStack() as whole:
        def sb(name, shape, dt=F32):
            return whole.enter_context(nc.sbuf_tensor(name, shape, dt))

        psum = whole.enter_context(nc.psum_tensor("psum", [P, BANKS, W], F32))
        common = {
            "x_hi": sb("x_hi", [P, X_KEPT, TG], F32R),
            "x_lo": sb("x_lo", [P, X_KEPT, TG], F32R),
            "x_raw": sb("x_raw", [P, 4, TG]),
            "mean_rstd": sb("mean_rstd", [P, 2, TG]),
            "stage": sb("stage", [P, 8, W]),
            "b_v": sb("b_v", [P, D]),
            "ident": sb("ident", [P, P]),
            "ones": sb("ones", [P, P]),
        }
        with ExitStack() as early:
            rows = early.enter_context(nc.sbuf_tensor("rows", [P, TG // P - 2, C], F32))
        with ExitStack() as a_memory:
            first = phase_a(nc, a_memory, whole, psum, common, rows, x, xT, Wqkv, bqkv, b_cols, A_T, WqT, keysT,
                        k_scr, q_scr, z_scr, v_scr, stat_scr, T, C, D, NE, RD, RANK, KT, TG, NG)
        second = phase_b(nc, whole, psum, common, first, x, Wo, bo, B_T, k_scr, q_scr, z_scr, v_scr, out,
                    T, C, D, S, QG, NQ, KEYT, DT)
        block = whole.enter_context(nc.Block())

        @block.sync
        def _(sp):
            first.sync(sp)
            second.sync(sp)

        @block.scalar
        def _(act):
            first.scalar(act)
            second.scalar(act)

        @block.tensor
        def _(pe):
            first.tensor(pe)
            second.tensor(pe)

        @block.gpsimd
        def _(pool):
            second.gpsimd(pool)

        @block.vector
        def _(dve):
            first.vector(dve)
            second.vector(dve)


class Programs:
    pass


def phase_a(nc, memory, whole, psum, common, rows, x, xT, Wqkv, bqkv, b_cols, A_T, WqT, keysT,
            k_scr, q_scr, z_scr, v_scr, stat_scr, T, C, D, NE, RD, RANK, KT, TG, NG):
    NTOK = TG // P
    HALF = TG // W
    IPP = KT // 2
    PRODUCTS = [("feature", lambda r: Wqkv[r, D:2 * D]), ("feature", lambda r: Wqkv[r, 0:D]),
                ("token", lambda r: A_T[r, :]), ("token", lambda r: Wqkv[r, 2 * D:3 * D])]
    IPG = IPP * len(PRODUCTS)
    RAW = 2
    ST = 8
    XS = 4
    M_R = 72
    STAT_STEPS = 5 * NTOK + 4
    GATE_STEPS = 4 * NTOK + 6
    EVA, EVD = 2 * NTOK + HALF + 1, 2 * NTOK
    EPS = 1e-5

    def order(product):
        if product == 1:
            return [2, 3, 4, 0, 1, 5, 6, 7]
        return [1, 2, 3, 4, 5, 0, 6, 7] if product == 2 else [*range(BANKS)]

    def sb(name, shape, dt=F32):
        return memory.enter_context(nc.sbuf_tensor(name, shape, dt))

    def sem(name):
        return whole.enter_context(nc.semaphore(name))

    x_raw, mean_rstd, stage, b_v = (common[n] for n in ("x_raw", "mean_rstd", "stage", "b_v"))
    ident, ones = common["ident"], common["ones"]
    x_rows = x_raw[:, 2:4, :].rearrange("p a b -> p (a b)")
    rq = x_raw[0:2 * RD, 0, :]
    x2_hi = sb("x2_hi", [P, KT - X_KEPT, TG], F32R)
    x2_lo = sb("x2_lo", [P, KT - X_KEPT, TG], F32R)
    w_hi = sb("w_hi", [P, RAW, 2, W], F32R)
    w_lo = sb("w_lo", [P, RAW, 2, W], F32R)
    score = sb("score", [P, NTOK, NE])
    left = sb("left", [P, NTOK, NE])
    w_raw = sb("w_raw", [P, RAW, 2, W])
    stats = sb("stats", [P, 4, 6])
    mv = sb("mv", [P, 2, NTOK])
    var = sb("var", [P, NTOK])
    std = sb("std", [P, NTOK])
    rs0 = sb("rs0", [P, NTOK])
    rs1 = sb("rs1", [P, NTOK])
    rs2 = sb("rs2", [P, NTOK])
    wq_raw = sb("wq_raw", [P, KT, RD])
    wq = sb("wq", [P, KT, M_R], F32R)
    keys2 = sb("keys2", [2 * RD, NE])
    top = sb("top", [P, NTOK, 8])
    top2 = sb("top2", [P, NTOK, 8])
    gsum = sb("gsum", [P, NTOK])
    b_kq = sb("b_kq", [P, 2, D // P])

    def first_rows(j):
        return rows[:, j - 1, :] if j < NTOK - 1 else stage[:, 0:4, :].rearrange("p a w -> p (a w)")

    def x_tile(part, k):
        if k < X_KEPT:
            return (common["x_hi"], common["x_lo"])[part][:, k, :]
        return (x2_hi, x2_lo)[part][:, k - X_KEPT, :]

    s_const = sem("s_const")
    s_wq = sem("s_wq")
    s_raw = [sem(f"s_raw{i}") for i in range(RAW)]
    s_whi = sem("s_whi")
    s_wlo = sem("s_wlo")
    s_used = sem("s_used")
    s_tile = sem("s_tile")
    s_rq = sem("s_rq")
    s_score = sem("s_score")
    s_evA = sem("s_evA")
    s_evD = sem("s_evD")
    s_out = [sem(f"s_out{i}") for i in range(ST)]
    s_rows = sem("s_rows")
    s_row0 = [sem(f"s_row0_{i}") for i in range(NTOK - 1)]
    s_ones = sem("s_ones")
    s_mv = sem("s_mv")
    s_stat = sem("s_stat")
    s_var = sem("s_var")
    s_std = sem("s_std")
    s_rstd = sem("s_rstd")
    s_diag = sem("s_diag")
    s_spread = sem("s_spread")
    s_stat0 = sem("s_stat0")
    s_mst = sem("s_mst")
    s_mld = sem("s_mld")
    s_xraw = [sem(f"s_xraw{i}") for i in range(XS)]
    s_xsub = sem("s_xsub")
    s_xn = sem("s_xn")
    s_xhi = sem("s_xhi")
    s_xlo = sem("s_xlo")
    s_gate = sem("s_gate")
    s_pass = sem("s_pass")
    s_gexp_in = sem("s_gexp_in")
    s_gexp = sem("s_gexp")

    stat_diag = [stage[:, ST // 2 + 2 * a:ST // 2 + 2 * a + 2, :].rearrange("p a (b q) -> p (a b) q", q=P)
                 for a in range(2)]

    w_rows = [slice(i * 2 * P, (i + 1) * 2 * P) for i in range(IPP)]

    def item(g, it):
        return g * IPG + it


    def taken(engine, g, product, j):
        if product < 2:
            wait(engine, s_evA, g * EVA + (NTOK + HALF if product else 0) + j + 1)
        else:
            wait(engine, s_evD, g * EVD + (NTOK if product == 3 else 0) + j + 1)

    def tile_ready(engine, g, product, pos):
        if pos < 7:
            engine.wait_ge(s_tile, g * 28 + product * 7 + pos + 1)
        else:
            engine.wait_ge(s_used, item(g, product * IPP + IPP - 1) + 1)

    def loop(engine, body):
        body(0, True)
        with engine.Fori(1, NG - 1) as g:
            body(g, True)
        body(NG - 1, False)

    def sync(sp):
        sp.wait_ge(s_row0[NTOK - 3], 16)

        def constants():
            sp.dma_start(wq_raw[:], WqT.rearrange("(k p) r -> p k r", p=P)).then_inc(s_const, 16)
            sp.dma_start(keys2[0:RD, :], keysT).then_inc(s_const, 16)
            sp.dma_start(keys2[RD:2 * RD, :], keysT).then_inc(s_const, 16)
            sp.dma_start(b_kq[:, 0, :], b_cols[:, D // P:2 * D // P]).then_inc(s_const, 16)
            sp.dma_start(b_kq[:, 1, :], b_cols[:, 0:D // P]).then_inc(s_const, 16)
            sp.dma_start(b_v[:], bqkv[2 * D:3 * D].rearrange("(a d) -> a d", a=1)
                         .to_broadcast([P, D])).then_inc(s_const, 16)

        def store(g, product):
            for pos, j in enumerate(order(product)):
                slot = pos % ST
                taken(sp, g, product, pos)
                if product < 2:
                    dst = (k_scr, q_scr)[product][(j // HALF) * P:(j // HALF + 1) * P,
                                                  bass.ds(g * TG + (j % HALF) * W, W)]
                else:
                    dst = (z_scr, v_scr)[product - 2][bass.ds(g * TG + j * P, P), :]
                sp.dma_start(dst, stage[:, slot, :]).then_inc(s_out[slot], 16)

        def body(g, more):
            for it in range(IPG):
                n = item(g, it)
                product, i = it // IPP, it % IPP
                wait(sp, s_wlo, n - RAW + 1)
                sp.dma_start(w_raw[:, it % RAW], PRODUCTS[product][1](w_rows[i])
                             .rearrange("(a p) w -> p a w", p=P)).then_inc(s_raw[it % RAW], 16)
                if it == 1 and static(g) and g == 0:
                    constants()
                if i == 1:
                    if product:
                        store(g, product - 1)
                    elif not (static(g) and g == 0):
                        store(g - 1, len(PRODUCTS) - 1)

        loop(sp, body)

    def last_store(sp):
        for pos in range(NTOK):
            slot = pos % ST
            taken(sp, NG - 1, 3, pos)
            sp.dma_start(v_scr[(NG - 1) * TG + pos * P:(NG - 1) * TG + (pos + 1) * P, :], stage[:, slot, :]
                         ).then_inc(s_out[slot], 16)

    def stored(engine, but):
        for slot in range(ST):
            engine.wait_ge(s_out[slot], 16 * (NG * 4 - but))

    def x_pair_load(act, g, pair):
        for k in (2 * pair, 2 * pair + 1):
            act.dma_start(x_raw[:, k % XS, :], xT[k * P:(k + 1) * P, bass.ds(g * TG, TG)]
                          ).then_inc(s_xraw[k % XS], 16)

    def rows_load(act, g, j):
        act.dma_start(x_rows, x[bass.ds(g * TG + j * P, P), :]).then_inc(s_rows, 16)

    def scalar(act):
        def split_weights(g, it):
            n = item(g, it)
            act.wait_ge(s_raw[it % RAW], 16 * (g * (IPG // RAW) + it // RAW + 1))
            wait(act, s_used, n - RAW + 1)
            nc.scalar.activation(w_hi[:, it % RAW], w_raw[:, it % RAW], ACT.Copy).then_inc(s_whi, 1)

        def take_features(g, product):
            for pos, j in enumerate(order(product)):
                slot = pos % ST
                tile_ready(act, g, product, pos)
                wait(act, s_out[slot], 16 * (g * 4 + product))
                nc.scalar.activation(stage[:, slot, :], psum[:, j, :], ACT.Identity,
                                     bias=b_kq[:, product, j // HALF:j // HALF + 1]).then_inc(s_evA, 1)

        def split_x_pair(g, pair):
            for k in (2 * pair, 2 * pair + 1):
                act.wait_ge(s_xn, g * KT + k + 1)
                wait(act, s_used, item(g - 1, 3 * IPP + pair) + 1)
                nc.scalar.activation(x_tile(0, k), x_raw[:, k % XS, :], ACT.Copy).then_inc(s_xhi, 1)

        def square_roots(g):
            act.wait_ge(s_var, g + 1)
            nc.scalar.activation(std[:], var[:], ACT.Sqrt).then_inc(s_std, 1)

        def store_stats(g):
            act.wait_ge(s_rstd, g + 1)
            for a in range(2):
                act.dma_start(stat_scr[bass.ds(g, 1), a, :].rearrange("o (j p) -> p (o j)", p=P),
                              mv[:, a, :], allow_slow_non_contiguous=True).then_inc(s_mst, 16)

        def broadcast_stats(g):
            act.wait_ge(s_mst, 32 * g)
            act.dma_start(mean_rstd[:].rearrange("p a t -> p (a t)"),
                          stat_scr[bass.ds(g, 1)].rearrange("o a t -> o (a t)")
                          .to_broadcast([P, 2 * TG])).then_inc(s_mld, 16)

        rows_load(act, 0, 0)
        for j in range(1, NTOK):
            act.dma_start(first_rows(j), x[j * P:(j + 1) * P, :]).then_inc(s_row0[j - 1], 16)
        x_pair_load(act, 0, 0)
        act.wait_ge(s_mv, 1)
        x_pair_load(act, 0, 1)
        square_roots(0)
        for a in range(2):
            act.wait_ge(s_spread, a + 1)
            nc.scalar.activation(mean_rstd[:, a, :], psum[:, 2 * a:2 * a + 2, :].rearrange("p a w -> p (a w)"),
                                 ACT.Copy).then_inc(s_stat0, 1)
            if a == 0:
                split_weights(0, 0)

        def body(g, more):
            first = static(g) and g == 0
            for it in range(IPG):
                product, i = it // IPP, it % IPP
                if it or not first:
                    split_weights(g, it)
                if it == IPP:
                    take_features(g, 0)
                    for h in range(HALF):
                        act.wait_ge(s_rq, g * HALF + h + 1)
                        nc.scalar.activation(rq[:, h * W:(h + 1) * W], psum[0:2 * RD, h, :],
                                             ACT.Copy).then_inc(s_evA, 1)
                if it == 2 * IPP:
                    take_features(g, 1)
                    act.wait_ge(s_score, g + 1)
                    nc.scalar.activation(score[:].rearrange("p j e -> p (j e)"), psum[:, 0, :],
                                         ACT.Copy).then_inc(s_evA, 1)
                if it == 2 * IPP + 2:
                    act.wait_ge(s_gexp_in, g + 1)
                    nc.scalar.activation(score[:], score[:], ACT.Exp).then_inc(s_gexp, 1)
                if first and it == 1:
                    act.wait_ge(s_const, 96)
                    act.wait_ge(s_wq, 1)
                    nc.scalar.activation(wq[:, :, 0:RD], wq_raw[:], ACT.Copy).then_inc(s_wq, 1)
                if first and it < IPP:
                    split_x_pair(0, it)
                    if it + 2 < IPP:
                        act.wait_ge(s_xlo, 2 * it + 2)
                        x_pair_load(act, 0, it + 2)
                elif it == 0:
                    split_x_pair(g, IPP - 1)
                if more:
                    if IPP - 1 <= it < IPP - 1 + NTOK:
                        if it == IPP - 1:
                            act.wait_ge(s_xlo, g * KT + KT)
                        else:
                            act.wait_ge(s_mv, (g + 1) * NTOK + it - IPP + 1)
                        rows_load(act, g + 1, it - IPP + 1)
                    if it == 2 * IPP + 1:
                        square_roots(g + 1)
                    if it == 2 * IPP + 3:
                        store_stats(g + 1)
                    if it == 2 * IPP + 4:
                        broadcast_stats(g + 1)
                        x_pair_load(act, g + 1, 0)
                        x_pair_load(act, g + 1, 1)
                    if it > 3 * IPP:
                        pair = it - 3 * IPP - 1
                        split_x_pair(g + 1, pair)
                        if pair + 2 < IPP:
                            act.wait_ge(s_xlo, (g + 1) * KT + 2 * pair + 2)
                            x_pair_load(act, g + 1, pair + 2)

        loop(act, body)

    def tensor(pe):
        def router(g):
            pe.wait_ge(s_wq, 3)
            for h in range(HALF):
                taken(pe, g, 0, h)
                for k in range(KT):
                    for part in range(2):
                        mm = pe.matmul(psum[0:M_R, h, :], wq[:, k, :], x_tile(part, k)[:, h * W:(h + 1) * W],
                                       start=(k == 0 and part == 0), stop=(k == KT - 1 and part == 1))
                mm.then_inc(s_rq, 1)

        def scores(g):
            taken(pe, g, 1, order(1).index(0))
            for j in range(NTOK):
                mm = pe.matmul(psum[:, 0, j * NE:(j + 1) * NE], rq[:, j * P:(j + 1) * P], keys2[:],
                               start=True, stop=True)
            mm.then_inc(s_score, 1)

        def bank_free(g, product, pos, j):
            if product == 0:
                taken(pe, g - 1, 3, pos)
            elif product == 1:
                if j < HALF:
                    wait(pe, s_evA, g * EVA + NTOK + j + 1)
                else:
                    taken(pe, g, 0, j)
            elif product == 2:
                if j == 0:
                    wait(pe, s_evA, g * EVA + EVA)
                else:
                    taken(pe, g, 1, order(1).index(j))
            else:
                taken(pe, g, 2, order(2).index(j))

        def body(g, more):
            for it in range(IPG):
                product, i = it // IPP, it % IPP
                slot = it % RAW
                pe.wait_ge(s_wlo, item(g, it) + 1)
                for a in range(2):
                    k = 2 * i + a
                    if product == 0:
                        pe.wait_ge(s_xlo, g * KT + k + 1)
                    for pos, j in enumerate(order(product)):
                        if k == 0:
                            if product == 0 and static(g) and g == 0:
                                if j < 4:
                                    pe.wait_ge(s_stat0, j // 2 + 1)
                            else:
                                bank_free(g, product, pos, j)
                        if PRODUCTS[product][0] == "feature":
                            m, h = j // HALF, j % HALF
                            wh, wl = (w[:, slot, a, m * P:(m + 1) * P] for w in (w_hi, w_lo))
                            xh, xl = (x_tile(part, k)[:, h * W:(h + 1) * W] for part in range(2))
                            parts = ((wh, xh), (wh, xl), (wl, xh))
                        else:
                            wh, wl = (w[:, slot, a, :] for w in (w_hi, w_lo))
                            xh, xl = (x_tile(part, k)[:, j * P:(j + 1) * P] for part in range(2))
                            parts = ((xh, wh), (xh, wl), (xl, wh))
                        for n, (stationary, moving) in enumerate(parts):
                            mm = pe.matmul(psum[:, j, :], stationary, moving,
                                           start=(k == 0 and n == 0), stop=(k == KT - 1 and n == 2))
                        if k == KT - 1 and pos < 7:
                            mm.then_inc(s_tile, 1)
                mm.then_inc(s_used, 1)
                if it == IPP - 1:
                    router(g)
                if it == 2 * IPP - 1:
                    scores(g)

        pe.wait_ge(s_ones, 2)
        for a in range(2):
            for j in range(NTOK):
                pe.wait_ge(s_diag, NTOK + 1 if a else j + 1)
                mm = pe.matmul(psum[:, 2 * a + j // 4, (j % 4) * P:(j % 4 + 1) * P], ones[:], stat_diag[a][:, j, :],
                               start=True, stop=True)
            mm.then_inc(s_spread, 1)
        loop(pe, body)

    def take_tokens(dve, g, product):
        for pos, j in enumerate(order(product)):
            slot = pos % ST
            tile_ready(dve, g, product, pos)
            wait(dve, s_out[slot], 16 * (g * 4 + product))
            if product == 2:
                ins = nc.vector.tensor_tensor(
                    stage[:, slot, :].rearrange("p (e r) -> p e r", r=RANK),
                    psum[:, j, :].rearrange("p (e r) -> p e r", r=RANK),
                    score[:, j, :].unsqueeze(2).to_broadcast([P, NE, RANK]), ALU.mult)
            else:
                ins = nc.vector.tensor_tensor(stage[:, slot, :], psum[:, j, :], b_v[:], ALU.add)
            ins.then_inc(s_evD, 1)

    def vector(dve):
        def split_weights(g, it):
            n = item(g, it)
            dve.wait_ge(s_whi, n + 1)
            nc.vector.tensor_tensor(w_lo[:, it % RAW], w_raw[:, it % RAW],
                                    w_hi[:, it % RAW].bitcast(F32), ALU.subtract).then_inc(s_wlo, 1)

        def normalise_pair(g, pair):
            def less_mean(k):
                if static(g) and g == 0 and k == 0:
                    dve.wait_ge(s_stat0, 1)
                dve.wait_ge(s_xraw[k % XS], 16 * (g * (KT // XS) + k // XS + 1))
                nc.vector.tensor_tensor(x_raw[:, k % XS, :], x_raw[:, k % XS, :], mean_rstd[:, 0, :],
                                        ALU.subtract).then_inc(s_xsub, 1)

            def over_std(k):
                if static(g) and g == 0 and k == 0:
                    dve.wait_ge(s_stat0, 2)
                dve.wait_ge(s_xsub, g * KT + k + 1)
                nc.vector.tensor_tensor(x_raw[:, k % XS, :], x_raw[:, k % XS, :], mean_rstd[:, 1, :],
                                        ALU.mult).then_inc(s_xn, 1)

            def low(k):
                dve.wait_ge(s_xhi, g * KT + k + 1)
                nc.vector.tensor_tensor(x_tile(1, k), x_raw[:, k % XS, :], x_tile(0, k).bitcast(F32),
                                        ALU.subtract).then_inc(s_xlo, 1)

            k = 2 * pair
            wait(dve, s_mld, 16 * g)
            if static(g) and g == 0 and pair == 0:
                less_mean(k)
                split_weights(g, 0)
                over_std(k)
                less_mean(k + 1)
                low(k)
                over_std(k + 1)
                low(k + 1)
            else:
                for step in (less_mean, over_std, low):
                    step(k)
                    step(k + 1)

        def stats_of_tile(g, j):
            chain = Chain(dve, s_stat, g * STAT_STEPS + 5 * j)
            if static(g) and g == 0 and j:
                dve.wait_ge(s_row0[j - 1], 16)
                source = first_rows(j)
            else:
                dve.wait_ge(s_rows, 16 if static(g) and g == 0 else 16 * ((g - 1) * NTOK + j + 2))
                source = x_rows
            for c in range(4):
                chain.step(nc.vector.bn_stats(stats[:, c, :], source[:, c * W:(c + 1) * W]))
            chain.wait()
            dve.sem_inc(s_pass, 1)
            chain.link(nc.vector.bn_aggr(mv[:, :, j], stats[:].rearrange("p a b -> p (a b)")))
            nc.vector.tensor_copy(var[:, j:j + 1], mv[:, 1, j:j + 1]).then_inc(s_mv, 1)
            if static(g) and g == 0:
                if j == 0:
                    dve.wait_ge(s_ones, 2)
                nc.vector.tensor_scalar(stat_diag[0][:, j, :], ident[:], mv[:, 0, j:j + 1], None,
                                        ALU.mult).then_inc(s_diag, 1)

        def rstd_ready(g):
            dve.wait_ge(s_mv, (g + 1) * NTOK)
            nc.vector.tensor_scalar(var[:], var[:], EPS, None, ALU.add).then_inc(s_var, 1)

        def rstd_finish(g):
            chain = Chain(dve, s_stat, g * STAT_STEPS + 5 * NTOK)
            dve.wait_ge(s_std, g + 1)
            chain.link(nc.vector.reciprocal(rs0[:], std[:]))
            chain.link(nc.vector.tensor_tensor(rs1[:], rs0[:], rs0[:], ALU.mult))
            chain.link(nc.vector.tensor_tensor(rs2[:], rs1[:], var[:], ALU.mult))
            chain.link(nc.vector.tensor_scalar(rs1[:], rs2[:], -0.5, 1.5, ALU.mult, ALU.add))
            nc.vector.tensor_tensor(mv[:, 1, :], rs0[:], rs1[:], ALU.mult).then_inc(s_rstd, 1)

        def pick_experts(g):
            chain = Chain(dve, s_gate, g * GATE_STEPS)
            dve.wait_ge(s_evA, g * EVA + EVA)
            dve.sem_inc(s_pass, 1)
            for j in range(NTOK):
                chain.step(nc.vector.max(top[:, j, :], score[:, j, :]))
            for j in range(NTOK):
                chain.wait(NTOK - 1)
                dve.sem_inc(s_pass, 1)
                chain.step(nc.vector.match_replace(left[:, j, :], top[:, j, :], score[:, j, :], LOWEST))
            for j in range(NTOK):
                chain.wait(NTOK - 1)
                dve.sem_inc(s_pass, 1)
                chain.step(nc.vector.max(top2[:, j, :], left[:, j, :]))
            for j in range(NTOK):
                chain.wait(NTOK - 1)
                dve.sem_inc(s_pass, 1)
                chain.step(nc.vector.match_replace(left[:, j, :], top2[:, j, :], left[:, j, :], LOWEST))
            chain.wait()
            chain.link(nc.vector.tensor_tensor(left[:], left[:], score[:], ALU.not_equal))
            nc.vector.tensor_tensor(score[:], score[:], top[:, :, 0:1].to_broadcast([P, NTOK, NE]),
                                    ALU.subtract).then_inc(s_gexp_in, 1)

        def finish_gates(g):
            chain = Chain(dve, s_gate, g * GATE_STEPS + 4 * NTOK + 1)
            dve.wait_ge(s_gexp, g + 1)
            chain.link(nc.vector.tensor_tensor(score[:], score[:], left[:], ALU.mult))
            chain.link(nc.vector.tensor_reduce(gsum[:], score[:], AX.X, ALU.add))
            chain.link(nc.vector.tensor_scalar(gsum[:], gsum[:], 0.5, None, ALU.mult))
            chain.link(nc.vector.reciprocal(gsum[:], gsum[:]))
            chain.link(nc.vector.tensor_tensor(score[:], score[:], gsum[:].unsqueeze(2)
                                               .to_broadcast([P, NTOK, NE]), ALU.mult))

        nc.vector.memset(ones[:], 1.0)
        nc.vector.memset(ident[:], 0.0).then_inc(s_ones, 1)
        nc.vector.memset(wq[:].bitcast(F32), 0.0).then_inc(s_wq, 1)
        for j in range(NTOK):
            stats_of_tile(0, j)
        rstd_ready(0)
        rstd_finish(0)
        dve.wait_ge(s_rstd, 1)
        nc.vector.tensor_tensor(stat_diag[1], ident[:].unsqueeze(1).to_broadcast([P, NTOK, P]),
                                mv[:, 1, :].unsqueeze(2).to_broadcast([P, NTOK, P]), ALU.mult).then_inc(s_diag, 1)

        def body(g, more):
            first = static(g) and g == 0
            for it in range(IPG):
                if it or not first:
                    split_weights(g, it)
                if it == 0 and not first:
                    take_tokens(dve, g - 1, 3)
                if it == 3 * IPP:
                    take_tokens(dve, g, 2)
                if first and it < IPP:
                    normalise_pair(0, it)
                    if it == 1:
                        dve.wait_ge(s_wq, 2)
                        nc.vector.tensor_tensor(wq[:, :, RD:2 * RD], wq_raw[:], wq[:, :, 0:RD].bitcast(F32),
                                                ALU.subtract).then_inc(s_wq, 1)
                elif it == 0:
                    normalise_pair(g, IPP - 1)
                if it == 2 * IPP:
                    pick_experts(g)
                if it == 2 * IPP + 4:
                    finish_gates(g)
                if more:
                    if IPP <= it < IPP + NTOK:
                        stats_of_tile(g + 1, it - IPP)
                    if it == 2 * IPP + 1:
                        rstd_ready(g + 1)
                    if it == 2 * IPP + 2:
                        rstd_finish(g + 1)
                    if it > 3 * IPP:
                        normalise_pair(g + 1, it - 3 * IPP - 1)

        loop(dve, body)

    def identity(pool):
        pool.wait_ge(s_ones, 1)
        nc.gpsimd.affine_select(out=ident[:], in_=ident[:], compare_op=ALU.not_equal, fill=1.0, base=0,
                                pattern=[[-1, P]], channel_multiplier=1).then_inc(s_ones, 1)

    first = Programs()
    first.sync, first.scalar, first.tensor, first.vector, first.gpsimd = sync, scalar, tensor, vector, identity
    first.last_store, first.stored, first.s_ones = last_store, stored, s_ones
    first.x_used = lambda engine: engine.wait_ge(s_used, item(NG - 1, 3 * IPP + 5) + 1)
    first.raw_used = lambda engine: engine.wait_ge(s_xlo, NG * KT)
    first.bank_taken = lambda engine, bank: taken(engine, NG - 1, 3, bank)
    first.take_last = lambda dve: take_tokens(dve, NG - 1, 3)
    return first


def phase_b(nc, whole, psum, common, first, x, Wo, bo, B_T, k_scr, q_scr, z_scr, v_scr, out,
            T, C, D, S, QG, NQ, KEYT, DT):
    RING = 4
    S_IT, O_IT, V_IT = KEYT // 2, 16, KEYT // 2
    PER = S_IT + O_IT + V_IT
    CB = C // W
    OPB = O_IT // CB
    QT = QG // P
    PR = 4
    XO = 8
    MISC = 7
    SCALE = float(D) ** -0.5
    S_BANK = [i % 7 for i in range(KEYT)]
    O_BANK = [i % 7 for i in range(CB * QT)]
    V_BANK = [2, 3, 4, 5]
    V_AFTER = [max(i for i, b in enumerate(O_BANK) if b == v) for v in V_BANK]
    S_LAST = [max(i for i, b in enumerate(S_BANK) if b == v) for v in range(7)]
    MAX_STEPS = KEYT - 1
    EXP_STEP = 4

    def sb(name, shape, dt=F32):
        return whole.enter_context(nc.sbuf_tensor(name, shape, dt))

    def sem(name):
        return whole.enter_context(nc.semaphore(name))

    def split_buffers(first, tiles, width):
        return [common[n][:, first:first + tiles, :].rearrange("p a (b w) -> p (a b) w", w=width)
                for n in ("x_hi", "x_lo")]

    r_raw = common["x_raw"]
    r_hi, r_lo = split_buffers(2, RING, 2 * W)
    q_raw = common["mean_rstd"][:].rearrange("p a (b w) -> p (a b) w", w=QG)
    q_hi, q_lo = split_buffers(0, 2, QG)
    p_hi, p_lo = split_buffers(6, 2, QG)
    f_hi, f_lo = split_buffers(8, 4, QG)
    attn = common["stage"][:, 0:DT, :]
    z_raw = common["stage"][:, DT:2 * DT, :]
    ident, ones = common["ident"], common["ones"]
    prob = sb("prob", [P, KEYT, QG])
    res = sb("res", [P, XO, W])
    b_out = sb("b_out", [P, C])
    run_max = sb("run_max", [P, QG])
    q_max = sb("q_max", [P, QT])
    diag = sb("diag", [P, QT, P])
    max_all = sb("max_all", [P, QG])
    run_sum = sb("run_sum", [P, QG])
    inv_sum = sb("inv_sum", [P, QG])

    b_const = sem("b_const")
    b_raw = [sem(f"b_raw{i}") for i in range(RING)]
    b_hi = sem("b_hi")
    b_lo = sem("b_lo")
    b_used = sem("b_used")
    b_q = sem("b_q")
    b_qhi = sem("b_qhi")
    b_qlo = sem("b_qlo")
    b_s = sem("b_s")
    b_copy = sem("b_copy")
    b_max = sem("b_max")
    b_tr = sem("b_tr")
    b_qmax = sem("b_qmax")
    b_diag = sem("b_diag")
    b_bc = sem("b_bc")
    b_mall = sem("b_mall")
    b_sub = sem("b_sub")
    b_exp = sem("b_exp")
    b_acc = sem("b_acc")
    b_sum = sem("b_sum")
    b_inv = sem("b_inv")
    b_phi = sem("b_phi")
    b_plo = sem("b_plo")
    b_pused = sem("b_pused")
    b_pv = sem("b_pv")
    b_attn = sem("b_attn")
    b_ahi = sem("b_ahi")
    b_alo = sem("b_alo")
    b_z = sem("b_z")
    b_zt = sem("b_zt")
    b_zhi = sem("b_zhi")
    b_zlo = sem("b_zlo")
    b_o = sem("b_o")
    b_oev = sem("b_oev")
    b_x = [sem(f"b_x{i}") for i in range(XO)]
    b_xb = sem("b_xb")
    b_st = [sem(f"b_st{i}") for i in range(XO)]

    def number(t, it):
        if static(t) and t == 0 and it < S_IT:
            return it
        if static(t) and t == NQ:
            return PER * NQ - O_IT + it - S_IT
        return PER * t - O_IT + it

    def uses(t, it):
        n = number(t, it)
        if static(n):
            return n // RING + 1
        return t * (PER // RING) + (it - O_IT) // RING + 1

    def segments(engine, scores, output, values):
        scores(0)
        values(0, True)
        scores(1)
        output(0, True)
        values(1, True)
        with engine.Fori(2, NQ - 1) as t:
            scores(t)
            output(t - 1, True)
            values(t, True)
        scores(NQ - 1)
        output(NQ - 2, True)
        values(NQ - 1, False)

    def score_ready(engine, t, i):
        if i % 2 == 0:
            engine.wait_ge(b_s, t * (KEYT // 2) + i // 2 + 1)
        else:
            engine.wait_ge(b_used, number(t, i // 2) + 1)

    def out_ready(engine, u, c, j):
        if j < QT - 1:
            engine.wait_ge(b_o, u * CB * (QT - 1) + c * (QT - 1) + j + 1)
        else:
            engine.wait_ge(b_used, number(u + 1, S_IT + c * OPB + OPB - 1) + 1)

    def sync(sp):
        def fetch(t, it, source):
            slot = it % RING
            wait(sp, b_lo, number(t, it) - RING + 1)
            sp.dma_start(r_raw[:, slot, :].rearrange("p (a w) -> p a w", a=source.shape[1]),
                         source).then_inc(b_raw[slot], 16)

        def queries(t):
            sp.dma_start(q_raw[:], q_scr.rearrange("(m p) t -> p m t", p=P)[:, :, bass.ds(t * QG, QG)]
                         ).then_inc(b_q, 16)

        def batch_base(t):
            return (t // (S // QG)) * S

        def store_block(u, c):
            for j in range(QT):
                slot = (c * QT + j) % XO
                sp.wait_ge(b_oev, u * CB * QT + c * QT + j + 1)
                sp.dma_start(out[bass.ds(u * QG + j * P, P), c * W:(c + 1) * W], res[:, slot, :]
                             ).then_inc(b_st[slot], 16)

        def load_block(u, c):
            for j in range(QT):
                slot = (c * QT + j) % XO
                wait(sp, b_st[slot], 16 * (u * (CB * QT // XO) + (c * QT + j) // XO))
                sp.dma_start(res[:, slot, :], x[bass.ds(u * QG + j * P, P), c * W:(c + 1) * W]
                             ).then_inc(b_x[slot], 16)

        def scores(t):
            base = batch_base(t)
            for i in range(S_IT):
                if static(t) and t == 0 and i == RING:
                    first.last_store(sp)
                    sp.dma_start(b_out[:], bo.rearrange("(a d) -> a d", a=1).to_broadcast([P, C])
                                 ).then_inc(b_const, 16)
                fetch(t, i, k_scr.rearrange("(m p) t -> p m t", p=P)[:, :, bass.ds(base + i * 2 * P, 2 * P)])

        def output(u, softmax):
            for i in range(O_IT):
                c, part = i // OPB, i % OPB
                source, row = (B_T, part * 2 * P) if part < OPB // 2 else (Wo, (part - OPB // 2) * 2 * P)
                fetch(u + 1, S_IT + i, source[row:row + 2 * P, c * W:(c + 1) * W]
                      .rearrange("(a p) w -> p a w", p=P))
                if part == 0 and c >= 2:
                    store_block(u, c - 2)
                if part == 1:
                    load_block(u, c)

        def values(t, more):
            base = batch_base(t)
            for i in range(V_IT):
                fetch(t, S_IT + O_IT + i, v_scr[bass.ds(base + i * 2 * P, 2 * P), :]
                      .rearrange("(a p) w -> p a w", p=P))
                if i == 0:
                    if static(t) and t == 0:
                        first.stored(sp, 0)
                    wait(sp, b_zt, QT * t)
                    sp.dma_start(z_raw[:], z_scr[bass.ds(t * QG, QG), :]
                                 .rearrange("(a p) w -> p a w", p=P)).then_inc(b_z, 16)
                    if more:
                        wait(sp, b_qlo, 2 * (t + 1))
                        queries(t + 1)
                if not (static(t) and t == 0):
                    if i == 0:
                        store_block(t - 1, CB - 2)
                    if i == 4:
                        store_block(t - 1, CB - 1)

        first.raw_used(sp)
        first.stored(sp, 1)
        queries(0)
        segments(sp, scores, output, values)
        output(NQ - 1, False)
        store_block(NQ - 1, CB - 2)
        store_block(NQ - 1, CB - 1)
        for slot in range(XO):
            sp.wait_ge(b_st[slot], 16 * NQ * CB * QT // XO)

    def scalar(act):
        def split(t, it):
            slot, n = it % RING, number(t, it)
            act.wait_ge(b_raw[slot], 16 * uses(t, it))
            wait(act, b_used, n - RING + 1)
            nc.scalar.activation(r_hi[:, slot, :], r_raw[:, slot, :], ACT.Copy).then_inc(b_hi, 1)

        def split_queries(t, half):
            act.wait_ge(b_q, 16 * (t + 1))
            wait(act, b_used, number(t - 1, S_IT - 1) + 1 if not (static(t) and t == 0) else 0)
            rows = slice(half * DT // 2, (half + 1) * DT // 2)
            nc.scalar.activation(q_hi[:, rows, :], q_raw[:, rows, :], ACT.Copy).then_inc(b_qhi, 1)

        def take_scores(t, i):
            score_ready(act, t, i)
            wait(act, b_plo, (t - 1) * KEYT + i + 1)
            wait(act, b_acc, t * (KEYT - 1))
            nc.scalar.activation(prob[:, i, :], psum[:, S_BANK[i], :], ACT.Copy).then_inc(b_copy, 1)

        def take_maximum(t):
            act.wait_ge(b_bc, t + 1)
            nc.scalar.activation(max_all[:], psum[:, MISC, :], ACT.Copy).then_inc(b_mall, 1)

        def exponential(t, i):
            act.wait_ge(b_sub, t * KEYT + i + 1)
            nc.scalar.activation(prob[:, i, :], prob[:, i, :], ACT.Exp, scale=SCALE).then_inc(b_exp, 1)

        def split_attention(t):
            for d in range(DT):
                act.wait_ge(b_attn, t * DT + d + 1)
                nc.scalar.activation(f_hi[:, d, :], attn[:, d, :], ACT.Copy).then_inc(b_ahi, 1)

        def split_z(t, m):
            act.wait_ge(b_zt, t * DT + m + 1)
            nc.scalar.activation(f_hi[:, DT + m, :], psum[:, MISC, :], ACT.Copy).then_inc(b_zhi, 1)

        def finish_values(t):
            split_z(t, DT - 1)
            split_attention(t)

        def scores(t):
            split(t, 0)
            for i in range(S_IT):
                if i + 1 < S_IT:
                    split(t, i + 1)
                if i == 0 and not (static(t) and t == 0):
                    finish_values(t - 1)
                if i >= 1:
                    take_scores(t, 2 * i - 2)
                    take_scores(t, 2 * i - 1)

        def softmax_step(t, i):
            if i == 0:
                take_scores(t, KEYT - 2)
                take_scores(t, KEYT - 1)
            if i == 3:
                take_maximum(t)
            if EXP_STEP <= i < EXP_STEP + KEYT // 2:
                exponential(t, 2 * (i - EXP_STEP))
                exponential(t, 2 * (i - EXP_STEP) + 1)

        def output(u, softmax):
            for i in range(O_IT):
                split(u + 1, S_IT + i)
                if softmax:
                    softmax_step(u + 1, i)
                elif i == 1:
                    finish_values(u)

        def softmax_start(t):
            softmax_step(t, 0)
            split(t, S_IT + O_IT)
            for i in range(1, EXP_STEP + 1):
                softmax_step(t, i)

        def softmax_ahead(t, i):
            for step in (EXP_STEP + 1 + 2 * i, EXP_STEP + 2 + 2 * i):
                softmax_step(t, step)

        def values(t, more):
            if static(t) and t == 0:
                softmax_start(t)
            for i in range(V_IT):
                if i or not (static(t) and t == 0):
                    split(t, S_IT + O_IT + i)
                for k in (2 * i, 2 * i + 1):
                    if k >= PR:
                        if k % 2 == 0:
                            act.wait_ge(b_pused, t * (KEYT // 2) + (k - PR) // 2 + 1)
                        else:
                            act.wait_ge(b_used, number(t, S_IT + O_IT + (k - PR) // 2) + 1)
                    act.wait_ge(b_exp, t * KEYT + k + 1)
                    nc.scalar.activation(p_hi[:, k % PR, :], prob[:, k, :], ACT.Copy).then_inc(b_phi, 1)
                if static(t) and t == 0:
                    softmax_ahead(t, i)
                if i >= 5:
                    split_z(t, i - 5)
                if more and i in (5, 6):
                    split_queries(t + 1, i - 5)

        first.x_used(act)
        split_queries(0, 0)
        split_queries(0, 1)
        segments(act, scores, output, values)
        output(NQ - 1, False)

    def tensor(pe):
        def three(bank, sh, sl, mh, ml, first, last):
            pe.matmul(bank, sh, mh, start=first, stop=False)
            pe.matmul(bank, sh, ml, start=False, stop=False)
            return pe.matmul(bank, sl, mh, start=False, stop=last)

        def streamed(t, it):
            pe.wait_ge(b_lo, number(t, it) + 1)
            return r_hi[:, it % RING, :], r_lo[:, it % RING, :]

        def scores(t):
            pe.wait_ge(b_qlo, 2 * (t + 1))
            for i in range(S_IT):
                kh, kl = streamed(t, i)
                for a in range(2):
                    tile = 2 * i + a
                    bank = S_BANK[tile]
                    if tile >= 7:
                        pe.wait_ge(b_copy, t * KEYT + tile - 7 + 1)
                    elif static(t) and t == 0:
                        first.bank_taken(pe, bank)
                    else:
                        if bank in V_BANK:
                            pe.wait_ge(b_attn, (t - 1) * DT + V_BANK.index(bank) + 1)
                        else:
                            wait(pe, b_oev, (t - 1) * CB * QT)
                    for d in range(DT):
                        cols = slice(d * 2 * P + a * P, d * 2 * P + (a + 1) * P)
                        mm = three(psum[:, bank, :], kh[:, cols], kl[:, cols],
                                   q_hi[:, d, :], q_lo[:, d, :], d == 0, d == DT - 1)
                    mm.then_inc((b_s, b_used)[a], 1)

        def transpose_maxima(t):
            pe.wait_ge(b_max, (t + 1) * MAX_STEPS)
            wait(pe, b_zlo, t * DT)
            for j in range(QT):
                mm = pe.transpose(psum[:, MISC, j * P:(j + 1) * P], run_max[:, j * P:(j + 1) * P], ident[:])
            mm.then_inc(b_tr, 1)

        def broadcast_maxima(t):
            pe.wait_ge(b_diag, (t + 1) * QT)
            for j in range(QT):
                mm = pe.matmul(psum[:, MISC, j * P:(j + 1) * P], ones[:], diag[:, j, :], start=True, stop=True)
            mm.then_inc(b_bc, 1)

        def total(t):
            pe.wait_ge(b_acc, (t + 1) * (KEYT - 1))
            pe.matmul(psum[:, MISC, :], ones[:], run_sum[:], start=True, stop=True).then_inc(b_sum, 1)

        def output(u, softmax):
            for c in range(CB):
                for part in range(OPB):
                    i = c * OPB + part
                    wh, wl = streamed(u + 1, S_IT + i)
                    attention = part >= OPB // 2
                    f0 = (part - OPB // 2) * 2 if attention else DT + 2 * part
                    if i < OPB // 2:
                        pe.wait_ge(b_zlo, u * DT + 2 * (i + 1))
                    if i == OPB // 2:
                        pe.wait_ge(b_alo, (u + 1) * DT)
                    for a in range(2):
                        for j in range(QT):
                            tile = c * QT + j
                            bank = O_BANK[tile]
                            if part == 0 and a == 0:
                                if tile >= 7:
                                    pe.wait_ge(b_oev, u * CB * QT + tile - 7 + 1)
                                elif softmax:
                                    pe.wait_ge(b_copy, (u + 1) * KEYT + S_LAST[bank] + 1)
                                else:
                                    pe.wait_ge(b_oev, u * CB * QT)
                                    if bank in V_BANK:
                                        pe.wait_ge(b_attn, u * DT + V_BANK.index(bank) + 1)
                            tok = slice(j * P, (j + 1) * P)
                            cols = slice(a * W, (a + 1) * W)
                            mm = three(psum[:, bank, :], f_hi[:, f0 + a, tok], f_lo[:, f0 + a, tok],
                                       wh[:, cols], wl[:, cols], part == 0 and a == 0,
                                       part == OPB - 1 and a == 1)
                            if part == OPB - 1 and a == 1 and j < QT - 1:
                                mm.then_inc(b_o, 1)
                    mm.then_inc(b_used, 1)
                    if softmax and i == 0:
                        transpose_maxima(u + 1)
                    if softmax and i == 2:
                        broadcast_maxima(u + 1)

        def values(t, more):
            if static(t) and t == 0:
                first.bank_taken(pe, MISC)
                transpose_maxima(t)
                broadcast_maxima(t)
            for i in range(V_IT):
                vh, vl = streamed(t, S_IT + O_IT + i)
                for a in range(2):
                    k = 2 * i + a
                    pe.wait_ge(b_plo, t * KEYT + k + 1)
                    for d in range(DT):
                        bank = V_BANK[d]
                        if k == 0:
                            if static(t) and t == 0:
                                pe.wait_ge(b_copy, S_LAST[bank] + 1)
                            else:
                                pe.wait_ge(b_oev, (t - 1) * CB * QT + V_AFTER[d] + 1)
                        cols = slice(a * W + d * P, a * W + (d + 1) * P)
                        mm = three(psum[:, bank, :], vh[:, cols], vl[:, cols], p_hi[:, k % PR, :],
                                   p_lo[:, k % PR, :], k == 0, k == KEYT - 1)
                        if k == KEYT - 1 and d < DT - 1:
                            mm.then_inc(b_pv, 1)
                    if a == 0:
                        mm.then_inc(b_pused, 1)
                mm.then_inc(b_used, 1)
                if i == 3:
                    total(t)
                if i >= 4:
                    m = i - 4
                    if m == 0:
                        pe.wait_ge(b_z, 16 * (t + 1))
                        pe.wait_ge(b_inv, t + 1)
                    else:
                        pe.wait_ge(b_zlo, t * DT + m)
                    for j in range(QT):
                        mm = pe.transpose(psum[:, MISC, j * P:(j + 1) * P],
                                          z_raw[:, j, m * P:(m + 1) * P], ident[:])
                    mm.then_inc(b_zt, 1)

        pe.wait_ge(first.s_ones, 2)
        segments(pe, scores, output, values)
        output(NQ - 1, False)

    def gpsimd(pool):
        first.gpsimd(pool)
        pool.wait_ge(b_const, 16)

        def add_bias(u, c):
            for j in range(QT):
                slot = (c * QT + j) % XO
                pool.wait_ge(b_x[slot], 16 * (u * (CB * QT // XO) + (c * QT + j) // XO + 1))
                nc.gpsimd.tensor_tensor(res[:, slot, :], res[:, slot, :], b_out[:, c * W:(c + 1) * W],
                                        ALU.add).then_inc(b_xb, 1)

        def sums(t, tiles):
            for i in tiles:
                pool.wait_ge(b_exp, t * KEYT + i + 1)
                if i == 1:
                    wait(pool, b_sum, t)
                    nc.gpsimd.tensor_tensor(run_sum[:], prob[:, 0, :], prob[:, 1, :], ALU.add).then_inc(b_acc, 1)
                else:
                    pool.wait_ge(b_acc, t * (KEYT - 1) + i - 1)
                    nc.gpsimd.tensor_tensor(run_sum[:], run_sum[:], prob[:, i, :], ALU.add).then_inc(b_acc, 1)

        def scores(t):
            pass

        def output(u, softmax):
            for c in range(CB):
                add_bias(u, c)
                if softmax and c < 3:
                    sums(u + 1, (range(1, 6), range(6, 12), range(12, KEYT))[c])

        def values(t, more):
            if static(t) and t == 0:
                sums(t, range(1, KEYT))

        segments(pool, scores, output, values)
        output(NQ - 1, False)

    def vector(dve):
        def split(t, it):
            slot = it % RING
            dve.wait_ge(b_hi, number(t, it) + 1)
            nc.vector.tensor_tensor(r_lo[:, slot, :], r_raw[:, slot, :], r_hi[:, slot, :].bitcast(F32),
                                    ALU.subtract).then_inc(b_lo, 1)

        def split_queries(t, half):
            dve.wait_ge(b_qhi, 2 * t + half + 1)
            rows = slice(half * DT // 2, (half + 1) * DT // 2)
            nc.vector.tensor_tensor(q_lo[:, rows, :], q_raw[:, rows, :], q_hi[:, rows, :].bitcast(F32),
                                    ALU.subtract).then_inc(b_qlo, 1)

        def maximum(t, i):
            dve.wait_ge(b_copy, t * KEYT + i + 1)
            if i == 1:
                nc.vector.tensor_tensor(run_max[:], prob[:, 0, :], prob[:, 1, :], ALU.max).then_inc(b_max, 1)
            elif i > 1:
                dve.wait_ge(b_max, t * MAX_STEPS + i - 1)
                nc.vector.tensor_tensor(run_max[:], run_max[:], prob[:, i, :], ALU.max).then_inc(b_max, 1)

        def query_maxima(t):
            dve.wait_ge(b_tr, t + 1)
            nc.vector.tensor_reduce(q_max[:], psum[:, MISC, :].rearrange("p (j k) -> p j k", j=QT), AX.X,
                                    ALU.max).then_inc(b_qmax, 1)
            dve.wait_ge(b_qmax, t + 1)
            for j in range(QT):
                nc.vector.tensor_scalar(diag[:, j, :], ident[:], q_max[:, j:j + 1], None,
                                        ALU.mult).then_inc(b_diag, 1)

        def less_maximum(t, i):
            dve.wait_ge(b_mall, t + 1)
            nc.vector.tensor_tensor(prob[:, i, :], prob[:, i, :], max_all[:], ALU.subtract).then_inc(b_sub, 1)

        def softmax_step(t, i):
            if i == 0:
                maximum(t, KEYT - 2)
                maximum(t, KEYT - 1)
            if i == 1:
                query_maxima(t)
            if EXP_STEP <= i < EXP_STEP + KEYT // 2:
                less_maximum(t, 2 * (i - EXP_STEP))
                less_maximum(t, 2 * (i - EXP_STEP) + 1)

        def take_attention(t):
            if static(t) and t == 0:
                first.stored(dve, 0)
            for d in range(DT):
                if d < DT - 1:
                    dve.wait_ge(b_pv, t * (DT - 1) + d + 1)
                else:
                    dve.wait_ge(b_used, number(t, PER - 1) + 1)
                dve.wait_ge(b_inv, t + 1)
                nc.vector.tensor_tensor(attn[:, d, :], psum[:, V_BANK[d], :], inv_sum[:],
                                        ALU.mult).then_inc(b_attn, 1)
            for d in range(DT):
                dve.wait_ge(b_ahi, t * DT + d + 1)
                nc.vector.tensor_tensor(f_lo[:, d, :], attn[:, d, :], f_hi[:, d, :].bitcast(F32),
                                        ALU.subtract).then_inc(b_alo, 1)

        def split_z(t, m):
            dve.wait_ge(b_zhi, t * DT + m + 1)
            nc.vector.tensor_tensor(f_lo[:, DT + m, :], psum[:, MISC, :], f_hi[:, DT + m, :].bitcast(F32),
                                    ALU.subtract).then_inc(b_zlo, 1)

        def finish_values(t):
            split_z(t, DT - 1)
            take_attention(t)

        def take_output(u, c):
            for j in range(QT):
                tile = c * QT + j
                out_ready(dve, u, c, j)
                dve.wait_ge(b_xb, u * CB * QT + tile + 1)
                nc.vector.tensor_tensor(res[:, tile % XO, :], psum[:, O_BANK[tile], :], res[:, tile % XO, :],
                                        ALU.add).then_inc(b_oev, 1)

        def scores(t):
            split(t, 0)
            for i in range(S_IT):
                if i + 1 < S_IT:
                    split(t, i + 1)
                if i == 0 and static(t) and t == 0:
                    first.take_last(dve)
                elif i == 0:
                    finish_values(t - 1)
                if i >= 1:
                    maximum(t, 2 * i - 2)
                    maximum(t, 2 * i - 1)

        def output(u, softmax):
            for i in range(O_IT):
                split(u + 1, S_IT + i)
                if i and i % OPB == 0:
                    take_output(u, i // OPB - 1)
                if softmax:
                    softmax_step(u + 1, i)
                elif i == 1:
                    finish_values(u)

        def softmax_start(t):
            softmax_step(t, 0)
            softmax_step(t, 1)
            split(t, S_IT + O_IT)
            for i in range(2, EXP_STEP + 1):
                softmax_step(t, i)

        def softmax_ahead(t, i):
            for step in (EXP_STEP + 1 + 2 * i, EXP_STEP + 2 + 2 * i):
                softmax_step(t, step)

        def values(t, more):
            if static(t) and t == 0:
                softmax_start(t)
            for i in range(V_IT):
                if i or not (static(t) and t == 0):
                    split(t, S_IT + O_IT + i)
                for k in (2 * i, 2 * i + 1):
                    dve.wait_ge(b_phi, t * KEYT + k + 1)
                    nc.vector.tensor_tensor(p_lo[:, k % PR, :], prob[:, k, :], p_hi[:, k % PR, :].bitcast(F32),
                                            ALU.subtract).then_inc(b_plo, 1)
                if static(t) and t == 0:
                    softmax_ahead(t, i)
                if i == 0 and not (static(t) and t == 0):
                    take_output(t - 1, CB - 1)
                if i == 4:
                    dve.wait_ge(b_sum, t + 1)
                    nc.vector.reciprocal(inv_sum[:], psum[:, MISC, :]).then_inc(b_inv, 1)
                if i >= 5:
                    split_z(t, i - 5)
                if more and i in (5, 6):
                    split_queries(t + 1, i - 5)

        split_queries(0, 0)
        split_queries(0, 1)
        segments(dve, scores, output, values)
        output(NQ - 1, False)
        take_output(NQ - 1, CB - 1)

    second = Programs()
    second.sync, second.scalar, second.tensor, second.gpsimd, second.vector = sync, scalar, tensor, gpsimd, vector
    return second


def kernel(L0_attn_x, L0_attn_Wqkv, L0_attn_bqkv, L0_attn_Wo, L0_attn_bo, L0_ffn_A_w, L0_ffn_B_w,
           L0_ffn_Wq_w, L0_ffn_keys):
    import numpy as np
    import concourse.bacc as bacc
    from concourse.bass_utils import run_bass_kernel_spmd

    B, S, C = L0_attn_x.shape
    x = np.ascontiguousarray(L0_attn_x).reshape(B * S, C)
    arrays = {
        "x": x,
        "xT": np.ascontiguousarray(x.T),
        "Wqkv": np.ascontiguousarray(L0_attn_Wqkv),
        "bqkv": np.ascontiguousarray(L0_attn_bqkv),
        "b_cols": np.ascontiguousarray(np.reshape(L0_attn_bqkv, (-1, P)).T),
        "Wo": np.ascontiguousarray(L0_attn_Wo),
        "bo": np.ascontiguousarray(L0_attn_bo),
        "A_T": np.ascontiguousarray(np.transpose(L0_ffn_A_w)),
        "B_T": np.ascontiguousarray(np.transpose(L0_ffn_B_w)),
        "WqT": np.ascontiguousarray(np.transpose(L0_ffn_Wq_w)),
        "keysT": np.ascontiguousarray(np.transpose(L0_ffn_keys)),
    }
    nc = bacc.Bacc("TRN2", target_bir_lowering=False, num_devices=1)
    args = [nc.dram_tensor(name, a.shape, mybir.dt.from_np(a.dtype), kind="ExternalInput").ap()
            for name, a in arrays.items()]
    out = nc.dram_tensor("out", [B * S, C], F32, kind="ExternalOutput").ap()
    layer_kernel(nc, *args, out)
    r = run_bass_kernel_spmd(nc, [arrays], core_ids=[0])
    return r.results[0]["out"].reshape(B, S, C)
```
